# Optimizing a Trainium2 kernel written in Bass

```python
import numpy as np
import jax
import jax.numpy as jnp

def _softmax(x, axis=-1):
    return jax.nn.softmax(x, axis=axis)

def _gelu(x):
    return jax.nn.gelu(x, approximate=True)

def _silu(x):
    return jax.nn.silu(x)

def _sigmoid(x):
    return jax.nn.sigmoid(x)

def _layernorm(x, axis=-1, eps=1e-05):
    m = jnp.mean(x, axis=axis, keepdims=True)
    v = jnp.var(x, axis=axis, keepdims=True)
    return (x - m) / jnp.sqrt(v + eps)

def _scatter_add(tgt, idx, src, axis=0):
    return tgt.at[idx].add(src)

def _segment_sum(src, seg, n):
    return jax.ops.segment_sum(src, seg, n)
kernel_name = 'mk_seq_preln_d1_jaxref_r8_b07d44'

def setup_inputs(seed: int=0):
    np.random.seed(seed)
    _w = jnp.asarray

    def _L0_attn_setup():
        import jax, jax.numpy as jnp
        import numpy as np
        B, S, D = (2, 128, 512)
        H, KVH, HD = (32, 8, 128)
        GROUPS = H // KVH
        LAT, LH = (128, 32)
        THETA = 10000.0
        SCALE = 1.0 / float(np.sqrt(HD))

        def _rope_cos_sin(seq_len, head_dim, theta):
            inv_freq = 1.0 / theta ** (jnp.arange(0, head_dim, 2, dtype=jnp.float32) / head_dim)
            t = jnp.arange(seq_len, dtype=jnp.float32)
            freqs = jnp.outer(t, inv_freq)
            emb = jnp.concatenate([freqs, freqs], axis=-1)
            return (jnp.cos(emb), jnp.sin(emb))

        def _rotate_half(x):
            h = x.shape[-1] // 2
            return jnp.concatenate([-x[..., h:], x[..., :h]], axis=-1)

        def _apply_rope(x, cos, sin):
            return x * cos[None, None] + _rotate_half(x) * sin[None, None]

        def _causal_attn(q, k, v, scale):
            s = jnp.einsum('bhqd,bhkd->bhqk', q, k) * scale
            mask = jnp.tril(jnp.ones((q.shape[2], k.shape[2]), dtype=bool))
            s = jnp.where(mask[None, None], s, jnp.finfo(s.dtype).min)
            p = jax.nn.softmax(s, axis=-1)
            return jnp.einsum('bhqk,bhkd->bhqd', p, v)
        key = jax.random.key(seed)
        ks = jax.random.split(key, 9)
        sd = 0.02
        mk = lambda k, shape: jax.random.normal(k, shape, dtype=jnp.float32) * sd
        return {'hidden_states': jax.random.normal(ks[0], (B, S, D), dtype=jnp.float32), 'w_q': mk(ks[1], (D, H * HD)), 'w_k': mk(ks[2], (D, KVH * HD)), 'w_v': mk(ks[3], (D, KVH * HD)), 'w_o': mk(ks[4], (H * HD, D)), 'w_lq': mk(ks[5], (D, LAT)), 'w_lk': mk(ks[6], (LAT, LH * HD)), 'w_lv': mk(ks[7], (D, LH * HD)), 'w_lo': mk(ks[8], (LH * HD, D))}
    _L0_attn_in = _L0_attn_setup()

    def _L0_ffn_setup():
        import jax, jax.numpy as jnp
        import numpy as np
        IMAGE_START_POS = 34
        Q_START = IMAGE_START_POS + 72 + 1
        Q_END = -1
        LORA_ALPHA = 32
        LORA_RANK = 16
        SCALING = LORA_ALPHA / LORA_RANK
        key = jax.random.key(seed)
        ks = jax.random.split(key, 7)
        B_, S, D, O, E, R = (4, 256, 512, 512, 8, LORA_RANK)
        s = 0.02
        return {'x': jax.random.normal(ks[0], (B_, S, D), jnp.float32), 'W': jax.random.normal(ks[1], (O, D), jnp.float32) * s, 'b': jax.random.normal(ks[2], (O,), jnp.float32) * s, 'A': jax.random.normal(ks[3], (E, R, D), jnp.float32) * s, 'B': jax.random.normal(ks[4], (E, O, R), jnp.float32) * s, 'router_W': jax.random.normal(ks[5], (E, D), jnp.float32) * s, 'router_b': jax.random.normal(ks[6], (E,), jnp.float32) * s}
    _L0_ffn_in = _L0_ffn_setup()
    _d = {'L0_attn_hidden_states': _L0_attn_in['hidden_states'], 'L0_attn_w_q': _L0_attn_in['w_q'], 'L0_attn_w_k': _L0_attn_in['w_k'], 'L0_attn_w_v': _L0_attn_in['w_v'], 'L0_attn_w_o': _L0_attn_in['w_o'], 'L0_attn_w_lq': _L0_attn_in['w_lq'], 'L0_attn_w_lk': _L0_attn_in['w_lk'], 'L0_attn_w_lv': _L0_attn_in['w_lv'], 'L0_attn_w_lo': _L0_attn_in['w_lo'], 'L0_ffn_W': _L0_ffn_in['W'], 'L0_ffn_b': _L0_ffn_in['b'], 'L0_ffn_A': _L0_ffn_in['A'], 'L0_ffn_B': _L0_ffn_in['B'], 'L0_ffn_router_W': _L0_ffn_in['router_W'], 'L0_ffn_router_b': _L0_ffn_in['router_b']}
    _x0 = _d['L0_attn_hidden_states']
    _d['L0_attn_hidden_states'] = jax.random.normal(jax.random.fold_in(jax.random.key(seed), 1), (1, 1024, 512), dtype=_x0.dtype)
    del _x0
    return _d

def reference(L0_attn_hidden_states, L0_attn_w_q, L0_attn_w_k, L0_attn_w_v, L0_attn_w_o, L0_attn_w_lq, L0_attn_w_lk, L0_attn_w_lv, L0_attn_w_lo, L0_ffn_W, L0_ffn_b, L0_ffn_A, L0_ffn_B, L0_ffn_router_W, L0_ffn_router_b):

    def _L0_attn_ref(hidden_states, w_q, w_k, w_v, w_o, w_lq, w_lk, w_lv, w_lo):
        import jax, jax.numpy as jnp
        import numpy as np
        B, S, D = (2, 128, 512)
        H, KVH, HD = (32, 8, 128)
        GROUPS = H // KVH
        LAT, LH = (128, 32)
        THETA = 10000.0
        SCALE = 1.0 / float(np.sqrt(HD))

        def _rope_cos_sin(seq_len, head_dim, theta):
            inv_freq = 1.0 / theta ** (jnp.arange(0, head_dim, 2, dtype=jnp.float32) / head_dim)
            t = jnp.arange(seq_len, dtype=jnp.float32)
            freqs = jnp.outer(t, inv_freq)
            emb = jnp.concatenate([freqs, freqs], axis=-1)
            return (jnp.cos(emb), jnp.sin(emb))

        def _rotate_half(x):
            h = x.shape[-1] // 2
            return jnp.concatenate([-x[..., h:], x[..., :h]], axis=-1)

        def _apply_rope(x, cos, sin):
            return x * cos[None, None] + _rotate_half(x) * sin[None, None]

        def _causal_attn(q, k, v, scale):
            s = jnp.einsum('bhqd,bhkd->bhqk', q, k) * scale
            mask = jnp.tril(jnp.ones((q.shape[2], k.shape[2]), dtype=bool))
            s = jnp.where(mask[None, None], s, jnp.finfo(s.dtype).min)
            p = jax.nn.softmax(s, axis=-1)
            return jnp.einsum('bhqk,bhkd->bhqd', p, v)
        x = hidden_states
        bsz, q_len, _ = x.shape
        q = (x @ w_q).reshape(bsz, q_len, H, HD).transpose(0, 2, 1, 3)
        k = (x @ w_k).reshape(bsz, q_len, KVH, HD).transpose(0, 2, 1, 3)
        v = (x @ w_v).reshape(bsz, q_len, KVH, HD).transpose(0, 2, 1, 3)
        lq = x @ w_lq
        lk = (lq @ w_lk).reshape(bsz, q_len, LH, HD).transpose(0, 2, 1, 3)
        lv = (x @ w_lv).reshape(bsz, q_len, LH, HD).transpose(0, 2, 1, 3)
        cos, sin = _rope_cos_sin(q_len, HD, THETA)
        q = _apply_rope(q, cos, sin)
        k = _apply_rope(k, cos, sin)
        lk = _apply_rope(lk, cos, sin)
        k = jnp.repeat(k, GROUPS, axis=1)
        v = jnp.repeat(v, GROUPS, axis=1)
        attn = _causal_attn(q, k, v, SCALE)
        lat = _causal_attn(q, lk, lv, SCALE)
        attn = attn.transpose(0, 2, 1, 3).reshape(bsz, q_len, H * HD)
        lat = lat.transpose(0, 2, 1, 3).reshape(bsz, q_len, LH * HD)
        return attn @ w_o + lat @ w_lo

    def _L0_ffn_ref(x, W, b, A, B, router_W, router_b):
        import jax, jax.numpy as jnp
        import numpy as np
        IMAGE_START_POS = 34
        Q_START = IMAGE_START_POS + 72 + 1
        Q_END = -1
        LORA_ALPHA = 32
        LORA_RANK = 16
        SCALING = LORA_ALPHA / LORA_RANK
        x_q = x[:, Q_START:Q_END, :]
        q = x_q.mean(axis=1)
        logits = q @ router_W.T + router_b
        routing = jax.nn.softmax(logits, axis=-1)
        base = x @ W.T + b
        t = jnp.einsum('bsd,erd->bser', x, A)
        lora = jnp.einsum('bser,eor,be->bso', t, B, routing) * SCALING
        return base + lora
    x = L0_attn_hidden_states
    x = x + _L0_attn_ref(_layernorm(x, axis=-1), L0_attn_w_q, L0_attn_w_k, L0_attn_w_v, L0_attn_w_o, L0_attn_w_lq, L0_attn_w_lk, L0_attn_w_lv, L0_attn_w_lo)
    x = x + _L0_ffn_ref(_layernorm(x, axis=-1), L0_ffn_W, L0_ffn_b, L0_ffn_A, L0_ffn_B, L0_ffn_router_W, L0_ffn_router_b)
    return x

_drawn_inputs = setup_inputs


def setup_inputs(seed=0):
    import zlib

    import numpy as np

    out = dict(_drawn_inputs(seed))
    spreads = {}
    factors = {'L0_attn_w_q': 6.015,
     'L0_attn_w_k': 6.091,
     'L0_attn_w_lq': 8.0,
     'L0_attn_w_lk': 8.0,
     'L0_ffn_b': 3.256,
     'L0_ffn_router_W': 64.0,
     'L0_ffn_router_b': 64.0,
     'L0_ffn_A': 2.911,
     'L0_ffn_B': 2.927}
    for name, (base, spread) in spreads.items():
        noise = np.random.default_rng([zlib.crc32(name.encode()), seed]).standard_normal(out[name].shape)
        drawn = base * np.exp(spread * noise) if base else spread * noise
        out[name] = jnp.asarray(drawn.astype(out[name].dtype))
    for name, factor in factors.items():
        out[name] = (out[name] * factor).astype(out[name].dtype)
    return out
```

```python
from contextlib import ExitStack

import numpy as np

import concourse.bass as bass
from concourse import mybir

F32 = mybir.dt.float32
F32R = mybir.dt.float32r
ALU = mybir.AluOpType
ACT = mybir.ActivationFunctionType
AX = mybir.AxisListType

P = 128
S, D = 1024, 512
H, KVH, HD = 32, 8, 128
E, R, O = 8, 16, 512
GROUP = H // KVH
NT, ND = S // P, D // P
CH = 512
TPC = CH // P
HALF = HD // 2
THETA = 10000.0
SCALE = 1.0 / float(np.sqrt(HD))
EPS = 1e-5
LORA_SCALING = 32 / 16
Q_START, Q_STOP = 34 + 72 + 1, S - 1
MASKED = -3.0e38

WINDOWS = [(0, 0), (0, 1), (1, 0), (1, 1)]
NW = len(WINDOWS)
BLOCKS = [TPC * (c + 1) for _, c in WINDOWS]
BLOCK0 = [sum(BLOCKS[:w]) for w in range(NW)]
BPH = sum(BLOCKS)
TILE_SLOTS = [[0, 0, 1, 2], [2, 3, 4, 5], [0, 0, 1, 2], [3, 4, 5, 6]]


def pieces_of(w, hh, more):
    if w == 0:
        names = [("LK", 0), ("LK", 1), ("LV", 0), ("LV", 1)]
        return dict(enumerate(names))
    if w == 1:
        return {0: ("LVT", 0), 1: ("LVT", 1), 2: ("OUT1", 0), 3: ("OUT1", 1), 4: ("OUT1", 2), 5: ("OUT1", 3)}
    if w == 2:
        if not more:
            return {}
        names = [("Q", 0), ("Q", 1)] + ([("K", 0), ("K", 1)] if hh == GROUP - 1 else [])
        return dict(enumerate(names))
    out = {4: ("OUT0", 0), 5: ("OUT0", 1), 6: ("OUT0", 2), 7: ("OUT0", 3)}
    if more and hh == GROUP - 1:
        out.update({0: ("V", 0), 1: ("V", 1), 2: ("VT", 0), 3: ("VT", 1)})
    return out


def number_pieces():
    at, n = {}, 0
    for hh in range(GROUP):
        for w in range(NW):
            for s, name in sorted(pieces_of(w, hh, True).items()):
                at[hh, w, s] = n
                n += 1
    return at, n


X_AT, XPG = number_pieces()
X_BEFORE = 10
ROPES_BEFORE = 4
ROPE = ("Q", "K", "LK")
ROPES_PER_GROUP = 2 * (2 * GROUP + 1)
VTS_PER_GROUP = 2 * (GROUP + 1)
LOADS_BEFORE = 6
LOADS_PER_GROUP = 5 * GROUP + 2

C_T, C_PV, C_B, C_OS, C_OL = 1, 3, 1, 1, 2


def p_offset(c, t):
    return P * sum(TPC * c + k + 1 for k in range(t))


def block_columns(c, j):
    return P * max(0, j - TPC * c)


def attn_ffn_kernel(nc, x_in, w_q, w_k, w_v, w_o, w_lq, w_lk, w_lv, w_out_latent, W, b, A, B, router_W, router_b,
                    cos_in, sin_in, mask_in, ident_in, pick_in, out):
    with ExitStack() as ctx:
        def sb(name, shape, dt=F32):
            return ctx.enter_context(nc.sbuf_tensor(name, shape, dt))

        def pair(name, shape):
            return sb(name + "_hi", shape, F32R), sb(name + "_lo", shape, F32R)

        def sem(name):
            return ctx.enter_context(nc.semaphore(name))

        cos = sb("cos", [P, S])
        sin = sb("sin", [P, S])
        mask = sb("mask", [P, S], mybir.dt.bfloat16)
        ident = sb("ident", [P, P])
        acc = sb("acc", [P, NT, D])
        xnT = pair("xnT", [P, ND, S])
        lqT = pair("lqT", [P, S])
        QT = pair("QT", [P, 2, S])
        KT = pair("KT", [P, S])
        LKT = pair("LKT", [P, S])
        V = pair("V", [P, NT, HD])
        LV = pair("LV", [P, NT, HD])
        vT = sb("vT", [P, S])
        probs = [sb(f"probs{c}", [P, p_offset(c, TPC)]) for c in range(2)]
        PT = pair("PT", [P, 2, CH])
        PTD = pair("PTD", [P, 2 * P])
        OT = pair("OT", [P, 2, S])
        o_raw = sb("o_raw", [P, 2, CH])
        inv_b = sb("inv_b", [P, CH])
        rot_a = sb("rot_a", [P, CH])
        rot_b = sb("rot_b", [P, CH])
        rot = sb("rot", [P, 2, CH])
        Wq = pair("Wq", [P, ND, HD])
        Wk = pair("Wk", [P, ND, HD])
        Wv = pair("Wv", [P, ND, HD])
        Wlv = pair("Wlv", [P, ND, HD])
        Wlk = pair("Wlk", [P, HD])
        Wo = pair("Wo", [P, D])
        Wlo = pair("Wlo", [P, D])
        stage = sb("stage", [P, 2, CH])
        nmax = sb("nmax", [P, 2, TPC])
        rsum = sb("rsum", [P, 2, TPC])
        rinv = sb("rinv", [P, 2, TPC])
        stats = sb("stats", [P, NT, 6])
        mv = sb("mv", [P, NT, 2])
        std = sb("std", [P, 4, NT])

        scores = [ctx.enter_context(nc.psum_tensor(f"scores{i}", [P, 2, CH], F32)) for i in range(2)]
        bankT = [ctx.enter_context(nc.psum_tensor(f"bankT{i}", [P, CH], F32)) for i in range(2)]
        bankO = ctx.enter_context(nc.psum_tensor("bankO", [P, CH], F32))
        bankX = ctx.enter_context(nc.psum_tensor("bankX", [P, CH], F32))

        x_loaded, consts_loaded, w_loaded = sem("x_loaded"), sem("consts_loaded"), [sem("w_loaded0"), sem("w_loaded1")]
        ffn_loaded, out_stored = sem("ffn_loaded"), sem("out_stored")
        scored, transposed, pv_done, x_ready = sem("scored"), sem("transposed"), sem("pv_done"), sem("x_ready")
        row_maxed, pt_lo, x_free, o_scaled, inverted = (sem("row_maxed"), sem("pt_lo"), sem("x_free"),
                                                        sem("o_scaled"), sem("inverted"))
        dve_step, act_step = sem("dve_step"), sem("act_step")
        exped, pt_hi, b_copied, w_hi, rope_hi, o_hi, v_hi = (sem("exped"), sem("pt_hi"), sem("b_copied"), sem("w_hi"),
                                                             sem("rope_hi"), sem("o_hi"), sem("v_hi"))
        rope_sum, rope_lo, o_lo, w_lo, cleared = (sem("rope_sum"), sem("rope_lo"), sem("o_lo"), sem("w_lo"),
                                                  sem("cleared"))
        xn_made, xt_ready, xt_hi, xt_lo = sem("xn_made"), sem("xt_ready"), sem("xt_hi"), sem("xt_lo")
        f_ready, f_hi, f_lo, f_free = sem("f_ready"), sem("f_hi"), sem("f_lo"), sem("f_free")
        y_done, f_chain, mask_made, score_seen = sem("y_done"), sem("f_chain"), sem("mask_made"), sem("score_seen")

        f32 = lambda ap: ap.bitcast(F32)

        def block_no(g, hh, w, j):
            return (g * GROUP + hh) * BPH + BLOCK0[w] + j

        def unit_no(g, hh, w):
            return (g * GROUP + hh) * NW + w

        def n_transposed(g, hh, w, j):
            return block_no(g, hh, w, j) + unit_no(g, hh, w) + 1 + C_T

        def n_piece(g, hh, w, s):
            skipped = 8 if isinstance(g, int) and g == KVH - 1 and (hh, w) == (GROUP - 1, NW - 1) else 0
            return g * XPG + (X_BEFORE + X_AT[hh, w, s] + 1 - skipped)

        def rope_no(g, hh, name, n):
            base = g * ROPES_PER_GROUP + (ROPES_BEFORE + 4 * hh)
            return base + {"LK": 0, "Q": 2, "K": 4}[name] + n

        def vt_no(g, hh, name, n):
            return g * VTS_PER_GROUP + (2 + 2 * hh + {"LVT": 0, "VT": 2}[name] + n)

        def load_no(g, hh, name):
            order = ["Wq"] + (["Wk", "Wv"] if hh == GROUP - 1 else []) + ["Wo", "Wlo", "Wlk", "Wlv"]
            return g * LOADS_PER_GROUP + (LOADS_BEFORE + 5 * hh + order.index(name))

        def n_latent_load(g, hh, name):
            before = g * LOADS_PER_GROUP + (LOADS_BEFORE + 5 * hh)
            return before - (1 if name == "Wlk" else 0)

        def tiles_made(g, hh, w):
            return TPC * (unit_no(g, hh, w) + 1)

        def last_block(g, hh, w):
            return block_no(g, hh, w, BLOCKS[w] - 1)

        def windows(g, last):
            for hh in range(GROUP):
                for w in range(NW):
                    yield hh, w, not (last and hh == GROUP - 1)

        def ring_slot(hh, w, j):
            ahead = sum(BLOCKS[k] - 1 for k in range(w)) + j
            return None if j == BLOCKS[w] - 1 else ahead % 2

        def pt_place(half, hh, w, j):
            slot = ring_slot(hh, w, j)
            if slot is None:
                return PTD[half][:, P:2 * P]
            return PT[half][:, slot, block_columns(WINDOWS[w][1], j):CH]

        def bank_no(hh, w, j):
            return (hh * (BPH + NW) + BLOCK0[w] + w + j) % 2

        def tile_view(ap, c):
            return ap if c == 0 else ap.rearrange("p (a n) -> p a n", a=2)

        def tile_bank(n, c, width):
            return scores[n % 2][:, 0, 0:width] if c == 0 else scores[n % 2][:, :, 0:width // 2]

        def prob_tile(c, t):
            width = P * (TPC * c + t + 1)
            return probs[c][:, p_offset(c, t):p_offset(c, t) + width]

        block = ctx.enter_context(nc.Block())

        @block.sync
        def _(sp):
            sp.dma_start(acc[:, :, :], x_in[0].rearrange("(i p) d -> p i d", p=P)).then_inc(x_loaded, 16)
            for place, src in ((ident, ident_in), (cos, cos_in), (sin, sin_in), (vT, mask_in)):
                sp.dma_start(place[:, :], src).then_inc(consts_loaded, 16)

            def load(no, slot, src):
                if not (isinstance(no, int) and no < 2):
                    sp.wait_ge(w_lo, no - 1)
                width = CH if len(src.shape) == 3 or src.shape[1] == CH else HD
                place = stage[:, slot, 0:width]
                if len(src.shape) == 3:
                    place = place.rearrange("p (k n) -> p k n", k=ND)
                sp.dma_start(place, src).then_inc(w_loaded[slot], 16)

            def columns(w, at):
                return w[:, bass.ds(at, HD)].rearrange("(k p) n -> p k n", p=P)

            for no, src in enumerate((columns(w_lq, 0), columns(w_q, 0), columns(w_k, 0), columns(w_v, 0),
                                      w_lk[:, 0:HD], columns(w_lv, 0))):
                load(no, no % 2, src)

            def group_of_heads(g, last):
                for hh in range(GROUP):
                    more = not (last and hh == GROUP - 1)
                    here = (g * GROUP + hh) * HD
                    after = (g * GROUP + hh + 1) * HD

                    def fetch(name, src):
                        no = load_no(g, hh, name)
                        load(no, load_no(0, hh, name) % 2, src)

                    if more:
                        fetch("Wq", columns(w_q, after))
                        if hh == GROUP - 1:
                            fetch("Wk", columns(w_k, (g + 1) * HD))
                            fetch("Wv", columns(w_v, (g + 1) * HD))
                    if not more:
                        for k, src in enumerate((w_o[bass.ds(here, HD), :], w_out_latent[bass.ds(here, HD), :])):
                            load(load_no(g, hh, "Wq") + k, (load_no(0, hh, "Wq") + k) % 2, src)
                        continue
                    fetch("Wo", w_o[bass.ds(here, HD), :])
                    fetch("Wlo", w_out_latent[bass.ds(here, HD), :])
                    fetch("Wlk", w_lk[:, bass.ds(after, HD)])
                    fetch("Wlv", columns(w_lv, after))

            with sp.Fori(0, KVH - 1) as g:
                group_of_heads(g, False)
            group_of_heads(KVH - 1, True)

            sp.wait_ge(x_ready, n_piece(KVH - 1, GROUP - 1, 1, 5))
            sp.wait_ge(transposed, n_transposed(KVH - 1, GROUP - 1, 3, BLOCKS[3] - 1))
            w_raw = probs[1][:, 0:ND * D].rearrange("p (k n) -> p k n", k=ND)
            sp.dma_start(w_raw, W.rearrange("(k p) n -> p k n", p=P)).then_inc(ffn_loaded, 16)
            sp.dma_start(probs[1][:, ND * D:ND * D + D], A.rearrange("e r d -> (e r) d")).then_inc(ffn_loaded, 16)
            b_raw = probs[1][:, ND * D + D:ND * D + 2 * D].rearrange("p (k e r) -> p k e r", k=ND, e=E)
            for k in range(ND):
                sp.dma_start(b_raw[:, k], B[:, k * P:(k + 1) * P, :].rearrange("e p r -> p e r"))\
                    .then_inc(ffn_loaded, 16)
            sp.dma_start(probs[0][0:E, 0:D], router_W).then_inc(ffn_loaded, 16)
            sp.dma_start(probs[0][:, D:2 * D], b.rearrange("(a n) -> a n", a=1).broadcast_to([P, D]))\
                .then_inc(ffn_loaded, 16)
            sp.dma_start(probs[0][:, 2 * D:2 * D + E],
                         router_b.rearrange("(a n) -> a n", a=1).broadcast_to([P, E])).then_inc(ffn_loaded, 16)
            sp.dma_start(probs[0][:, 2 * D + E:2 * D + 2 * E], pick_in).then_inc(ffn_loaded, 16)
            for i in range(NT):
                sp.wait_ge(y_done, i + 1)
                sp.dma_start(out[0, i * P:(i + 1) * P, :], acc[:, i, :]).then_inc(out_stored, 16)
            sp.wait_ge(out_stored, 16 * NT)

        n_ffn_loads = 6 + ND
        W_raw = probs[1][:, 0:ND * D].rearrange("p (k n) -> p k n", k=ND)
        A_raw = probs[1][:, ND * D:ND * D + D]
        B_raw = probs[1][:, ND * D + D:ND * D + 2 * D].rearrange("p (k c) -> p k c", k=ND)
        rw_raw = probs[0][0:E, 0:D]
        bias = probs[0][:, D:2 * D]
        r_bias = probs[0][:, 2 * D:2 * D + E]
        pick = probs[0][:, 2 * D + E:2 * D + 2 * E]
        WT = [h[:, :, :].rearrange("p a b -> p (a b)").rearrange("p (k n) -> p k n", k=ND) for h in OT]
        AT = [h[:, 0:CH].rearrange("p (k n) -> p k n", k=ND) for h in LKT]
        BT = [h[:, 0:O] for h in KT]
        rwT = rot_a[:, 0:ND * E].rearrange("p (k e) -> p k e", k=ND)
        tT = lqT
        xsum = rot_b[:, 0:ND]
        soft = rot_b[:, 64:64 + 8 * E].rearrange("p (k e) -> p k e", e=E)

        @block.tensor
        def _(pe):
            def mm3(place, left, right, start, stop):
                pe.matmul(place, left[1], right[0], start=start, stop=False)
                pe.matmul(place, left[0], right[1], start=False, stop=False)
                return pe.matmul(place, left[0], right[0], start=False, stop=stop)

            def both(pair_, *index):
                return [h[index] for h in pair_]

            ALL = slice(None)

            def normalised_transposes(made, ready):
                for i in range(NT):
                    pe.wait_ge(xn_made, made + i + 1)
                    if i >= 2 or made:
                        pe.wait_ge(xt_lo, made + i - 1)
                    for k in range(ND):
                        mm = pe.transpose(bankT[i % 2][:, k * P:(k + 1) * P],
                                          o_raw[:, i % 2, k * P:(k + 1) * P], ident[:, :])
                    mm.then_inc(ready, 1)

            def project(weights, n):
                for k in range(ND):
                    mm = mm3(bankX[:, :], both(weights, ALL, k, ALL), both(xnT, ALL, k, slice(n * CH, n * CH + CH)),
                             k == 0, k == ND - 1)
                return mm

            def value_transposes(n):
                for i in range(TPC):
                    mm = pe.transpose(bankX[:, i * P:(i + 1) * P],
                                      vT[:, (n * TPC + i) * P:(n * TPC + i + 1) * P], ident[:, :])
                return mm

            def out_tile(c, i):
                rows = slice((TPC * c + i) * P, (TPC * c + i + 1) * P)
                mm3(bankX[:, :], both(OT, ALL, 0, rows), both(Wo, ALL, ALL), True, False)
                return mm3(bankX[:, :], both(OT, ALL, 1, rows), both(Wlo, ALL, ALL), False, True)

            def score_tile(no, parity, head, kind, c, t):
                if not (isinstance(no, int) and no < 2):
                    pe.wait_ge(row_maxed, no - 1)
                i = TPC * c + t
                width = (i + 1) * P
                keys = LKT if kind else KT
                query = both(QT, ALL, head % 2, slice(i * P, (i + 1) * P))
                if c == 0:
                    n = max(width, 2 * P)
                    mm = mm3(scores[parity][:, 0, 0:n], query, both(keys, ALL, slice(0, n)), True, True)
                else:
                    for a in range(2):
                        part = slice(a * width // 2, (a + 1) * width // 2)
                        mm = mm3(scores[parity][:, a, 0:width // 2], query, both(keys, ALL, part), True, True)
                mm.then_inc(scored, 1)

            def transpose_block(g, hh, w, j):
                c = WINDOWS[w][1]
                no = block_no(g, hh, w, j)
                if j == 0:
                    pe.wait_ge(exped, tiles_made(g, hh, w))
                if j == 1:
                    pe.wait_ge(b_copied, unit_no(g, hh, w) + C_B)
                elif not (isinstance(no, int) and no == 0):
                    pe.wait_ge(pt_lo, no if j == 0 else no - 1)
                for t in range(max(0, j - TPC * c), TPC):
                    at = p_offset(c, t) + j * P
                    mm = pe.transpose(bankT[bank_no(hh, w, j)][:, t * P:(t + 1) * P],
                                      probs[c][:, at:at + P], ident[:, :])
                mm.then_inc(transposed, 1)

            def transpose_sums(g, hh, w):
                c = WINDOWS[w][1]
                pe.wait_ge(inverted, unit_no(g, hh, w) + 1)
                pe.wait_ge(pt_lo, last_block(g, hh, w))
                for t in range(TPC):
                    mm = pe.transpose(bankT[bank_no(hh, w, BLOCKS[w])][:, t * P:(t + 1) * P],
                                      rinv[:, c, t:t + 1].broadcast_to([P, P]), ident[:, :])
                mm.then_inc(transposed, 1)

            def pv_block(g, hh, w, j):
                kind, c = WINDOWS[w]
                no = block_no(g, hh, w, j)
                pe.wait_ge(pt_lo, no + 1)
                if j == 0:
                    pe.wait_ge(o_scaled, unit_no(g, hh, w) + C_OS)
                values = both(LV if kind else V, ALL, j, ALL)
                if j == BLOCKS[w] - 1:
                    mm = mm3(bankO[:, CH - 2 * P:CH], values, both(PTD, ALL, ALL), False, True)
                else:
                    at = block_columns(c, j)
                    mm = mm3(bankO[:, at:CH], values, both(PT, ALL, ring_slot(hh, w, j), slice(at, CH)), j == 0, False)
                mm.then_inc(pv_done, 1)

            def piece(g, hh, w, s, name, n):
                pe.wait_ge(x_free, n_piece(g, hh, w, s) - 1)
                if name == "LK":
                    pe.wait_ge(w_lo, n_latent_load(g, hh, "Wlk"))
                    mm = mm3(bankX[:, :], both(Wlk, ALL, ALL), both(lqT, ALL, slice(n * CH, n * CH + CH)), True, True)
                elif name == "LV":
                    pe.wait_ge(w_lo, n_latent_load(g, hh, "Wlv"))
                    mm = project(Wlv, n)
                elif name in ("LVT", "VT"):
                    mm = value_transposes(n)
                elif name == "Q":
                    pe.wait_ge(w_lo, load_no(g, hh, "Wq") + 1)
                    mm = project(Wq, n)
                elif name == "K":
                    pe.wait_ge(w_lo, load_no(g, hh, "Wk") + 1)
                    mm = project(Wk, n)
                elif name == "V":
                    pe.wait_ge(w_lo, load_no(g, hh, "Wv") + 1)
                    mm = project(Wv, n)
                elif name == "OUT0":
                    pe.wait_ge(w_lo, out_weights(g, hh, g_last[0]))
                    pe.wait_ge(o_lo, unit_no(g, hh, 2) + 1 + C_OL)
                    mm = out_tile(0, n)
                else:
                    pe.wait_ge(o_lo, unit_no(g, hh, 0) + C_OL)
                    mm = out_tile(1, n)
                mm.then_inc(x_ready, 1)

            g_last = [False]

            def out_weights(g, hh, last):
                if last and hh == GROUP - 1:
                    return load_no(g, hh, "Wq") + 2
                return load_no(g, hh, "Wlo") + 1

            def group_of_heads(g, last):
                g_last[0] = last
                for hh, w, more in windows(g, last):
                    nw, nhh = (w + 1) % NW, hh + (w == NW - 1)
                    for s in range(BLOCKS[w]):
                        if more or w < NW - 1:
                            for t in range(TPC):
                                if TILE_SLOTS[w][t] != s:
                                    continue
                                no = tiles_made(g, hh, w) + t
                                if t == 0 and w == 1:
                                    pe.wait_ge(rope_lo, rope_no(g, hh, "LK", 1) + 1)
                                if t == 0 and w == 3:
                                    pe.wait_ge(rope_lo, rope_no(g, hh, "K" if hh == GROUP - 1 else "Q", 1) + 1)
                                score_tile(no, t % 2, nhh, WINDOWS[nw][0], WINDOWS[nw][1], t)
                        if s + 1 < BLOCKS[w]:
                            transpose_block(g, hh, w, s + 1)
                        else:
                            transpose_sums(g, hh, w)
                        if s in pieces_of(w, hh, more):
                            piece(g, hh, w, s, *pieces_of(w, hh, more)[s])
                        if s == 0 and w in (0, 2):
                            if w == 2:
                                pe.wait_ge(x_free, n_piece(g, hh, 1, 1))
                            elif hh == 0:
                                pe.wait_ge(x_free, g * XPG + X_BEFORE)
                        pv_block(g, hh, w, s)
                    if nhh < GROUP:
                        transpose_block(g, nhh, nw, 0)
                    elif more:
                        transpose_block(g + 1, 0, 0, 0)

            pe.sem_inc(transposed, C_T)
            pe.sem_inc(pv_done, C_PV)
            pe.wait_ge(consts_loaded, 64)
            normalised_transposes(0, xt_ready)
            pe.wait_ge(xt_lo, NT)
            for x, (weights, n) in enumerate([(Wlv, 0), (Wlv, 1), (Wq, 0), (Wq, 1), (Wk, 0), (Wk, 1), (Wv, 0), (Wv, 1)]):
                pe.wait_ge(w_lo, x // 2 + 1)
                if x:
                    pe.wait_ge(x_free, x)
                project(weights, n).then_inc(x_ready, 1)
            for n in range(2):
                pe.wait_ge(x_free, 8 + n)
                value_transposes(n).then_inc(x_ready, 1)
            pe.wait_ge(rope_lo, ROPES_BEFORE)
            for t in range(TPC):
                score_tile(t, t % 2, 0, 0, 0, t)
            transpose_block(0, 0, 0, 0)

            with pe.Fori(0, KVH - 1) as g:
                group_of_heads(g, False)
            group_of_heads(KVH - 1, True)

            n_loop = n_piece(KVH - 1, GROUP - 1, 1, 5) + 4
            for n in range(TPC):
                pe.wait_ge(x_free, n_loop + n)
                if n == 0:
                    pe.wait_ge(o_lo, H * NW + C_OL)
                out_tile(1, n).then_inc(x_ready, 1)

            pe.wait_ge(ffn_loaded, 16 * n_ffn_loads)
            jobs = []
            for k in range(ND):
                jobs.append([(bankT, m, W_raw[:, m, k * P:(k + 1) * P]) for m in range(ND)])
            jobs.append([(bankT, k, A_raw[:, k * P:(k + 1) * P]) for k in range(ND)])
            jobs.append([(bankT, k, B_raw[:, k, :]) for k in range(ND)])
            pe.wait_ge(b_copied, H * NW + C_B)
            pe.wait_ge(pt_lo, H * BPH)
            for n, job in enumerate(jobs):
                if n >= 2:
                    pe.wait_ge(f_lo, n - 1)
                for banks, m, src in job:
                    mm = pe.transpose(banks[n % 2][:, m * P:(m + 1) * P], src, ident[:, :])
                mm.then_inc(f_ready, 1)
            pe.wait_ge(f_lo, len(jobs) - 1)
            for k in range(ND):
                mm = pe.transpose(bankT[0][:, k * E:(k + 1) * E], rw_raw[:, k * P:(k + 1) * P], ident[0:E, 0:E])
            mm.then_inc(f_ready, 1)
            pe.wait_ge(f_lo, len(jobs) + 1)
            normalised_transposes(NT, xt_ready)
            pe.wait_ge(xt_lo, 2 * NT)
            for n in range(2):
                for k in range(ND):
                    mm = mm3(scores[0][:, n, :], both(AT, ALL, k, ALL),
                             both(xnT, ALL, k, slice(n * CH, n * CH + CH)), k == 0, k == ND - 1)
                mm.then_inc(f_ready, 1)
            pe.wait_ge(f_lo, len(jobs) + 2)
            for k in range(ND):
                mm = pe.matmul(bankO[:, 0:E], xsum[:, k:k + 1].broadcast_to([P, P]), rwT[:, k, :],
                               start=(k == 0), stop=(k == ND - 1))
            mm.then_inc(f_ready, 1)
            pe.wait_ge(f_lo, len(jobs) + 4)
            for i in range(NT):
                place = scores[1][:, i % 2, :]
                if i >= 2:
                    pe.wait_ge(y_done, i - 1)
                rows = slice(i * P, (i + 1) * P)
                for k in range(ND):
                    mm3(place, both(xnT, ALL, k, rows), both(WT, ALL, k, ALL), k == 0, False)
                mm3(place, both(tT, ALL, rows), BT, False, True).then_inc(f_ready, 1)

        @block.scalar
        def _(act):
            def copy(place, src):
                return act.activation(place, src, ACT.Copy)

            def root(step):
                act.wait_ge(dve_step, step)
                act.activation(std[:, 1, :], std[:, 0, :], ACT.Sqrt).then_inc(act_step, 1)

            def normalised_hi(made):
                for i in range(NT):
                    act.wait_ge(xt_ready, made + i + 1)
                    copy(xnT[0][:, :, i * P:(i + 1) * P], bankT[i % 2][:, :].rearrange("p (k n) -> p k n", k=ND))\
                        .then_inc(xt_hi, 1)

            def weights_hi(no, slot, per_slot, places):
                act.wait_ge(w_loaded[slot], 16 * per_slot)
                place = places[0]
                src = stage[:, slot, 0:HD if places is Wlk else CH]
                if len(place.shape) == 3:
                    copy(place[:, :, :], src.rearrange("p (k n) -> p k n", k=ND)).then_inc(w_hi, 1)
                else:
                    copy(place[:, :], src).then_inc(w_hi, 1)

            def fetched(g, hh, name, places, at=None):
                no = load_no(0, hh, name) if at is None else at
                weights_hi(None, no % 2, g * (LOADS_PER_GROUP // 2) + (no // 2 + 1), places)

            def rope_high(no, parity, place):
                act.wait_ge(rope_sum, no + 1)
                copy(place, rot[:, parity, :]).then_inc(rope_hi, 1)

            def value_high(n_x, place, n):
                act.wait_ge(x_ready, n_x)
                copy(place[:, n * TPC:(n + 1) * TPC, :], bankX[:, :].rearrange("p (k n) -> p k n", k=TPC))\
                    .then_inc(v_hi, 1)

            def exp_tile(no, c, t):
                act.wait_ge(row_maxed, no + 1)
                act.activation(prob_tile(c, t), prob_tile(c, t), ACT.Exp, bias=nmax[:, c, t:t + 1], scale=-1.0,
                               accum_out=rsum[:, c, t:t + 1]).then_inc(exped, 1)

            def block_hi(g, hh, w, j):
                no = block_no(g, hh, w, j)
                c = WINDOWS[w][1]
                if not (isinstance(no, int) and no == 0):
                    ahead = 2 if (j < 2 or j == BLOCKS[w] - 1) else 1
                    act.wait_ge(pv_done, no - ahead + C_PV)
                else:
                    act.wait_ge(cleared, 1)
                act.wait_ge(transposed, n_transposed(g, hh, w, j))
                copy(pt_place(0, hh, w, j), bankT[bank_no(hh, w, j)][:, block_columns(c, j):CH]).then_inc(pt_hi, 1)

            def sums_copy(g, hh, w):
                act.wait_ge(o_scaled, unit_no(g, hh, w) + C_OS)
                act.wait_ge(transposed, n_transposed(g, hh, w, BLOCKS[w]))
                copy(inv_b[:, :], bankT[bank_no(hh, w, BLOCKS[w])][:, :]).then_inc(b_copied, 1)

            def group_of_heads(g, last):
                for hh, w, more in windows(g, last):
                    nw, nhh = (w + 1) % NW, hh + (w == NW - 1)
                    kind, c = WINDOWS[w]
                    third = last and hh == GROUP - 1
                    for s in range(BLOCKS[w]):
                        if s + 1 < BLOCKS[w]:
                            block_hi(g, hh, w, s + 1)
                        else:
                            sums_copy(g, hh, w)
                        if more or w < NW - 1:
                            for t in range(TPC):
                                if TILE_SLOTS[w][t] == s:
                                    exp_tile(tiles_made(g, hh, w) + t, WINDOWS[nw][1], t)
                        if w == 0 and s >= 2:
                            if s == 2:
                                act.wait_ge(scored, tiles_made(g, hh, 0))
                            no = rope_no(g, hh, "LK", s - 2)
                            rope_high(no, s % 2, LKT[0][:, (s - 2) * CH:(s - 1) * CH])
                        if w == 1 and s < 2:
                            if s == 0:
                                act.wait_ge(pv_done, last_block(g, hh, 0) + 1 + C_PV)
                            value_high(n_piece(g, hh, 1, s), LV[0], s)
                        if w == 1 and s == 6 and more:
                            act.wait_ge(x_ready, n_piece(g, hh, 0, 3))
                            fetched(g, hh, "Wq", Wq)
                            if hh == GROUP - 1:
                                fetched(g, hh, "Wk", Wk)
                        if w == 1 and s == 7 and more and hh == GROUP - 1:
                            fetched(g, hh, "Wv", Wv)
                        if w == 2 and s >= 2 and more:
                            if s == 2:
                                act.wait_ge(scored, tiles_made(g, hh, 2))
                            rope_high(rope_no(g, hh, "Q", s - 2), s % 2,
                                      QT[0][:, (hh + 1) % 2, (s - 2) * CH:(s - 1) * CH])
                        if w == 3 and s < 2:
                            if more and hh == GROUP - 1:
                                rope_high(rope_no(g, hh, "K", s), s % 2, KT[0][:, s * CH:(s + 1) * CH])
                            if s == 0:
                                act.wait_ge(x_ready, n_piece(g, hh, 1, 5))
                            name, places = (("Wo", Wo), ("Wlo", Wlo))[s]
                            fetched(g, hh, name, places, load_no(0, hh, "Wq") + s if third else None)
                        if w == 3 and s in (2, 3) and more and hh == GROUP - 1:
                            if s == 2:
                                act.wait_ge(pv_done, last_block(g, hh, 1) + 1 + C_PV)
                            value_high(n_piece(g, hh, 3, s), V[0], s - 2)
                        if w == 3 and s >= 6 and more:
                            name, places = (("Wlk", Wlk), ("Wlv", Wlv))[s - 6]
                            fetched(g, hh, name, places)
                    if nhh < GROUP:
                        block_hi(g, nhh, nw, 0)
                    elif more:
                        block_hi(g + 1, 0, 0, 0)
                    act.wait_ge(x_ready, n_piece(g, hh, *((0, 3) if c == 0 else (1, 5))))
                    act.wait_ge(o_scaled, unit_no(g, hh, w) + 1 + C_OS)
                    copy(OT[0][:, kind, c * CH:(c + 1) * CH], o_raw[:, w % 2, :]).then_inc(o_hi, 1)

            act.sem_inc(b_copied, C_B)
            root(1)
            normalised_hi(0)
            for no, places in enumerate((Wlv, Wq, Wk, Wv)):
                weights_hi(no, no % 2, no // 2 + 1, places)
            for n in range(2):
                act.wait_ge(x_ready, n + 1)
                copy(lqT[0][:, n * CH:(n + 1) * CH], bankX[:, :]).then_inc(v_hi, 1)
            weights_hi(4, 0, 3, Wlk)
            weights_hi(5, 1, 3, Wlv)
            for p in range(ROPES_BEFORE):
                n = p % 2
                rope_high(p, n, (QT[0][:, 0, n * CH:(n + 1) * CH], KT[0][:, n * CH:(n + 1) * CH])[p // 2])
            for n in range(2):
                value_high(9 + n, V[0], n)
            for t in range(TPC):
                exp_tile(t, 0, t)
            block_hi(0, 0, 0, 0)

            with act.Fori(0, KVH - 1) as g:
                group_of_heads(g, False)
            group_of_heads(KVH - 1, True)

            for n in range(ND + 2):
                act.wait_ge(f_ready, n + 1)
                if n == 0:
                    act.wait_ge(x_ready, n_piece(KVH - 1, GROUP - 1, 1, 5) + 8)
                src = bankT[n % 2][:, :]
                if n < ND:
                    copy(WT[0][:, n, :], src).then_inc(f_hi, 1)
                elif n == ND:
                    copy(AT[0], src.rearrange("p (k n) -> p k n", k=ND)).then_inc(f_hi, 1)
                else:
                    copy(BT[0], src).then_inc(f_hi, 1)
            root(3)
            normalised_hi(NT)
            act.wait_ge(f_free, 1)
            act.activation(soft[:, 2, :], soft[:, 0, :], ACT.Exp, bias=soft[:, 1, 0:1], scale=1.0,
                           accum_out=soft[:, 1, 1:2]).then_inc(act_step, 1)
            for n in range(2):
                act.wait_ge(f_free, 2 + n)
                copy(tT[0][:, n * CH:(n + 1) * CH], o_raw[:, n, :]).then_inc(f_hi, 1)

        @block.vector
        def _(dve):
            def statistics(step):
                if step:
                    dve.wait_ge(y_free_sem, y_free_count)
                for i in range(NT):
                    dve.bn_stats(stats[:, i, :], acc[:, i, :]).then_inc(dve_chain, 1)
                chain[0] += NT
                dve.wait_ge(dve_chain, chain[0])
                for i in range(NT):
                    dve.bn_aggr(mv[:, i, :], stats[:, i, :]).then_inc(dve_chain, 1)
                chain[0] += NT
                dve.wait_ge(dve_chain, chain[0])
                dve.tensor_scalar(std[:, 0, :], mv[:, :, 1], EPS, None, ALU.add).then_inc(dve_step, 1)
                dve.wait_ge(act_step, step // 2 + 1)
                link(dve.reciprocal(std[:, 2, :], std[:, 1, :]))
                link(dve.tensor_tensor(std[:, 3, :], std[:, 2, :], std[:, 0, :], ALU.mult))
                link(dve.tensor_tensor(std[:, 2, :], std[:, 3, :], std[:, 1, :], ALU.add))
                link(dve.tensor_scalar(std[:, 3, :], std[:, 2, :], 0.5, None, ALU.mult))
                dve.reciprocal(std[:, 2, :], std[:, 3, :]).then_inc(dve_step, 1)
                dve.wait_ge(dve_step, step + 2)

            chain = [0]
            dve_chain = f_chain
            y_free_sem, y_free_count = x_free, n_piece(KVH - 1, GROUP - 1, 1, 5) + 8

            def link(ins):
                chain[0] += 1
                ins.then_inc(dve_chain, 1)
                dve.wait_ge(dve_chain, chain[0])

            def normalise(made):
                for i in range(NT + 1):
                    if i < NT:
                        if i >= 2:
                            dve.wait_ge(xt_ready, made + i - 1)
                        dve.tensor_scalar(o_raw[:, i % 2, :], acc[:, i, :], mv[:, i, 0:1], std[:, 2, i:i + 1],
                                          ALU.subtract, ALU.mult).then_inc(xn_made, 1)
                    if i:
                        j = i - 1
                        dve.wait_ge(xt_hi, made + j + 1)
                        rows = slice(j * P, (j + 1) * P)
                        dve.tensor_tensor(xnT[1][:, :, rows], bankT[j % 2][:, :].rearrange("p (k n) -> p k n", k=ND),
                                          f32(xnT[0][:, :, rows]), ALU.subtract).then_inc(xt_lo, 1)

            def row_max(no, parity, c, t):
                dve.wait_ge(scored, no + 1)
                dve.sem_inc(score_seen, 1)
                width = P * (TPC * c + t + 1)
                place = tile_view(prob_tile(c, t), c)
                src = scores[parity][:, 0, 0:width] if c == 0 else scores[parity][:, :, 0:width // 2]
                dve.tensor_tensor_reduce(place, src, tile_view(mask[:, S - width:S], c), -SCALE, -MASKED,
                                         ALU.add, ALU.min, nmax[:, c, t:t + 1]).then_inc(row_maxed, 1)

            def block_lo(g, hh, w, j):
                c = WINDOWS[w][1]
                dve.wait_ge(pt_hi, block_no(g, hh, w, j) + 1)
                dve.tensor_tensor(pt_place(1, hh, w, j), bankT[bank_no(hh, w, j)][:, block_columns(c, j):CH],
                                  f32(pt_place(0, hh, w, j)), ALU.subtract).then_inc(pt_lo, 1)

            def rotate(n_x, no, n):
                if not (isinstance(no, int) and no == 0):
                    dve.wait_ge(rope_sum, no)
                dve.wait_ge(x_ready, n_x)
                t = slice(n * CH, (n + 1) * CH)
                dve.tensor_tensor(rot_a[:, :], bankX[:, :], cos[:, t], ALU.mult)
                dve.tensor_tensor(rot_b[0:HALF, :], bankX[HALF:HD, :], sin[HALF:HD, t], ALU.mult)
                dve.tensor_tensor(rot_b[HALF:HD, :], bankX[0:HALF, :], sin[0:HALF, t], ALU.mult).then_inc(x_free, 1)

            def value_copy(n_x, n):
                dve.wait_ge(x_ready, n_x)
                dve.tensor_copy(vT[:, n * CH:(n + 1) * CH], bankX[:, :]).then_inc(x_free, 1)

            def value_lo(n_v, places, n):
                dve.wait_ge(v_hi, n_v)
                rows = slice(n * TPC, (n + 1) * TPC)
                dve.tensor_tensor(places[1][:, rows, :], bankX[:, :].rearrange("p (k n) -> p k n", k=TPC),
                                  f32(places[0][:, rows, :]), ALU.subtract).then_inc(x_free, 1)

            def add_out(n_x, i):
                dve.wait_ge(x_ready, n_x)
                dve.wait_ge(x_free, n_x - 1)
                dve.tensor_tensor(acc[:, i, :], bankX[:, :], acc[:, i, :], ALU.add).then_inc(x_free, 1)

            def piece(g, hh, w, s, name, n):
                n_x = n_piece(g, hh, w, s)
                if name in ROPE:
                    rotate(n_x, rope_no(g, hh, name, n), n)
                elif name in ("V", "LV"):
                    value_copy(n_x, n)
                elif name in ("VT", "LVT"):
                    value_lo(vt_no(g, hh, name, n) + 3, V if name == "VT" else LV, n)
                else:
                    add_out(n_x, n + (TPC if name == "OUT1" else 0))

            def scale_out(g, hh, w):
                unit = unit_no(g, hh, w)
                dve.wait_ge(o_lo, unit - 1 + C_OL)
                dve.wait_ge(pv_done, last_block(g, hh, w) + 1 + C_PV)
                dve.wait_ge(b_copied, unit + 1 + C_B)
                dve.tensor_tensor(o_raw[:, w % 2, :], bankO[:, :], inv_b[:, :], ALU.mult).then_inc(o_scaled, 1)

            def group_of_heads(g, last):
                for hh, w, more in windows(g, last):
                    nw, nhh = (w + 1) % NW, hh + (w == NW - 1)
                    c = WINDOWS[w][1]
                    for s in range(BLOCKS[w]):
                        if s == 0:
                            dve.wait_ge(exped, tiles_made(g, hh, w))
                            dve.reciprocal(rinv[:, c, :], rsum[:, c, :]).then_inc(inverted, 1)
                        if more or w < NW - 1:
                            for t in range(TPC):
                                if TILE_SLOTS[w][t] == s:
                                    if t == 0:
                                        dve.wait_ge(transposed, block_no(g, hh, w, 0) + unit_no(g, hh, w) + C_T)
                                    row_max(tiles_made(g, hh, w) + t, t % 2, WINDOWS[nw][1], t)
                        if s + 1 < BLOCKS[w]:
                            block_lo(g, hh, w, s + 1)
                        if s in pieces_of(w, hh, more):
                            piece(g, hh, w, s, *pieces_of(w, hh, more)[s])
                    if nhh < GROUP:
                        block_lo(g, nhh, nw, 0)
                    elif more:
                        block_lo(g + 1, 0, 0, 0)
                    scale_out(g, hh, w)

            dve.sem_inc(o_scaled, C_OS)
            dve.wait_ge(consts_loaded, 64)
            dve.tensor_copy(mask[:, :], vT[:, :]).then_inc(mask_made, 1)
            dve.wait_ge(x_loaded, 16)
            statistics(0)
            normalise(0)
            for n in range(2):
                dve.wait_ge(v_hi, n + 1)
                dve.tensor_tensor(lqT[1][:, n * CH:(n + 1) * CH], bankX[:, :], f32(lqT[0][:, n * CH:(n + 1) * CH]),
                                  ALU.subtract).then_inc(x_free, 1)
            for p in range(ROPES_BEFORE):
                rotate(3 + p, p, p % 2)
            dve.wait_ge(mask_made, 1)
            for n in range(2):
                value_copy(7 + n, n)
            for n in range(2):
                value_lo(3 + n, V, n)
            dve.wait_ge(mask_made, 1)
            for t in range(TPC):
                row_max(t, t % 2, 0, t)
            block_lo(0, 0, 0, 0)

            with dve.Fori(0, KVH - 1) as g:
                group_of_heads(g, False)
            group_of_heads(KVH - 1, True)

            n_loop = n_piece(KVH - 1, GROUP - 1, 1, 5) + 4
            for n in range(TPC):
                add_out(n_loop + n + 1, TPC + n)
            for n in range(ND + 2):
                dve.wait_ge(f_hi, n + 1)
                src = bankT[n % 2][:, :]
                if n < ND:
                    hi, lo = f32(WT[0][:, n, :]), WT[1][:, n, :]
                elif n == ND:
                    hi, lo = f32(AT[0]), AT[1]
                    src = src.rearrange("p (k n) -> p k n", k=ND)
                else:
                    hi, lo = f32(BT[0]), BT[1]
                dve.tensor_tensor(lo, src, hi, ALU.subtract).then_inc(f_lo, 1)
            dve.wait_ge(f_ready, ND + 3)
            dve.tensor_copy(rwT, bankT[0][:, 0:ND * E].rearrange("p (k e) -> p k e", k=ND)).then_inc(f_lo, 1)
            statistics(2)
            normalise(NT)
            dve.wait_ge(xt_lo, 2 * NT)
            link(dve.tensor_reduce(xsum, f32(xnT[0][:, :, Q_START:Q_STOP]), AX.X, ALU.add))
            link(dve.tensor_reduce(rot_b[:, ND:2 * ND], f32(xnT[1][:, :, Q_START:Q_STOP]), AX.X, ALU.add))
            link(dve.tensor_tensor(rot_b[:, 2 * ND:3 * ND], xsum, rot_b[:, ND:2 * ND], ALU.add))
            dve.tensor_scalar(xsum, rot_b[:, 2 * ND:3 * ND], 1.0 / (Q_STOP - Q_START), None, ALU.mult)\
                .then_inc(f_lo, 1)
            for i in range(NT):
                dve.tensor_tensor(acc[:, i, :], acc[:, i, :], bias, ALU.add).then_inc(dve_chain, 1)
            chain[0] += NT
            dve.wait_ge(f_ready, ND + 6)
            link(dve.tensor_tensor(soft[:, 0, :], bankO[:, 0:E], r_bias, ALU.add))
            link(dve.tensor_reduce(soft[:, 1, 2:3], soft[:, 0, :], AX.X, ALU.max))
            dve.tensor_scalar(soft[:, 1, 0:1], soft[:, 1, 2:3], -1.0, None, ALU.mult).then_inc(f_free, 1)
            dve.wait_ge(act_step, 3)
            link(dve.reciprocal(soft[:, 1, 3:4], soft[:, 1, 1:2]))
            link(dve.tensor_tensor(soft[:, 3, :], soft[:, 2, :], pick, ALU.mult))
            link(dve.tensor_reduce(soft[:, 4, 0:1], soft[:, 3, :], AX.X, ALU.add))
            link(dve.tensor_scalar(soft[:, 4, 1:2], soft[:, 4, 0:1], soft[:, 1, 3:4], LORA_SCALING, ALU.mult, ALU.mult))
            for n in range(2):
                dve.tensor_scalar(o_raw[:, n, :], scores[0][:, n, :], soft[:, 4, 1:2], None, ALU.mult)\
                    .then_inc(f_free, 1)
            for n in range(2):
                dve.wait_ge(f_hi, ND + 3 + n)
                t = slice(n * CH, (n + 1) * CH)
                dve.tensor_tensor(tT[1][:, t], o_raw[:, n, :], f32(tT[0][:, t]), ALU.subtract).then_inc(f_lo, 1)
            for i in range(NT):
                dve.wait_ge(f_ready, ND + 6 + i + 1)
                dve.wait_ge(dve_chain, chain[0])
                dve.tensor_tensor(acc[:, i, :], scores[1][:, i % 2, :], acc[:, i, :], ALU.add).then_inc(y_done, 1)

        @block.gpsimd
        def _(pool):
            def subtract(place, src, hi):
                return pool.tensor_tensor(place, src, f32(hi), ALU.subtract)

            def rope_add(no, parity):
                if not (isinstance(no, int) and no < 2):
                    pool.wait_ge(rope_lo, no - 1)
                pool.wait_ge(x_free, rope_free(no))
                pool.tensor_tensor(rot[:, parity, :], rot_a[:, :], rot_b[:, :], ALU.add).then_inc(rope_sum, 1)

            rope_x = {}

            def rope_free(no):
                return rope_x["n"]

            def rope_low(no, parity, places, at):
                pool.wait_ge(rope_hi, no + 1)
                subtract(places[1][at], rot[:, parity, :], places[0][at]).then_inc(rope_lo, 1)

            def weights_low(no, slot, places):
                pool.wait_ge(w_hi, no + 1)
                src = stage[:, slot, 0:HD if places is Wlk else CH]
                if len(places[0].shape) == 3:
                    subtract(places[1][:, :, :], src.rearrange("p (k n) -> p k n", k=ND), places[0][:, :, :])\
                        .then_inc(w_lo, 1)
                else:
                    subtract(places[1][:, :], src, places[0][:, :]).then_inc(w_lo, 1)

            def ropes(g, hh, w, s0, name, places, at):
                for n in range(2):
                    rope_x["n"] = n_piece(g, hh, w, s0 + n)
                    rope_add(rope_no(g, hh, name, n), n)
                for n in range(2):
                    rope_low(rope_no(g, hh, name, n), n, places, at(n))

            ALL = slice(None)

            def chunk(n):
                return slice(n * CH, (n + 1) * CH)

            def out_low(g, hh, w):
                kind, c = WINDOWS[w]
                pool.wait_ge(o_hi, unit_no(g, hh, w) + 1)
                at = (ALL, kind, chunk(c))
                subtract(OT[1][at], o_raw[:, w % 2, :], OT[0][at]).then_inc(o_lo, 1)

            def group_of_heads(g, last):
                for hh, w, more in windows(g, last):
                    if w == 0:
                        ropes(g, hh, 0, 0, "LK", LKT, lambda n: (ALL, chunk(n)))
                    if w == 1 and more:
                        names = [("Wq", Wq)] + ([("Wk", Wk), ("Wv", Wv)] if hh == GROUP - 1 else [])
                        for name, places in names:
                            weights_low(load_no(g, hh, name), load_no(0, hh, name) % 2, places)
                    if w == 2 and more:
                        ropes(g, hh, 2, 0, "Q", QT, lambda n: (ALL, (hh + 1) % 2, chunk(n)))
                        if hh == GROUP - 1:
                            ropes(g, hh, 2, 2, "K", KT, lambda n: (ALL, chunk(n)))
                    if w == 3:
                        if more:
                            for name, places in (("Wo", Wo), ("Wlo", Wlo), ("Wlk", Wlk), ("Wlv", Wlv)):
                                weights_low(load_no(g, hh, name), load_no(0, hh, name) % 2, places)
                        else:
                            for k, places in enumerate((Wo, Wlo)):
                                weights_low(load_no(g, hh, "Wq") + k, (load_no(0, hh, "Wq") + k) % 2, places)
                    out_low(g, hh, w)

            pool.sem_inc(o_lo, C_OL)
            for tensor in (*PTD, *OT, *Wo, *Wlo):
                flat = tensor[tuple([ALL] * len(tensor.shape))]
                ins = pool.memset(f32(flat), 0.0)
            ins.then_inc(cleared, 1)
            for no, places in enumerate((Wlv, Wq, Wk, Wv)):
                weights_low(no, no % 2, places)
            weights_low(4, 0, Wlk)
            weights_low(5, 1, Wlv)
            for p in (0, 2):
                for n in range(2):
                    rope_x["n"] = 3 + p + n
                    rope_add(p + n, n)
                for n in range(2):
                    rope_low(p + n, n, (QT, KT)[p // 2], ((ALL, 0, chunk(n)), (ALL, chunk(n)))[p // 2])

            with pool.Fori(0, KVH - 1) as g:
                group_of_heads(g, False)
            group_of_heads(KVH - 1, True)


_INS = ["L0_attn_hidden_states", "L0_attn_w_q", "L0_attn_w_k", "L0_attn_w_v", "L0_attn_w_o", "L0_attn_w_lq",
        "L0_attn_w_lk", "L0_attn_w_lv", "L0_attn_w_lo", "L0_ffn_W", "L0_ffn_b", "L0_ffn_A", "L0_ffn_B",
        "L0_ffn_router_W", "L0_ffn_router_b"]


def shape_constants():
    inv_freq = (1.0 / THETA ** (np.arange(0, HD, 2, dtype=np.float32) / HD)).astype(np.float32)
    freqs = np.outer(np.arange(S, dtype=np.float32), inv_freq).astype(np.float32)
    cos = np.tile(np.cos(freqs).T, (2, 1)).astype(np.float32)
    sin = np.concatenate([np.sin(freqs).T, -np.sin(freqs).T], 0).astype(np.float32)
    mask = np.zeros((P, S), np.float32)
    mask[:, S - P:] = np.where(np.tril(np.ones((P, P), bool)), 0.0, MASKED)
    pick = (np.arange(P)[:, None] // R == np.arange(E)[None, :]).astype(np.float32)
    return {"cos": cos, "sin": sin, "mask": mask, "ident": np.eye(P, dtype=np.float32), "pick": pick}


def kernel(**inputs):
    import concourse.bacc as bacc
    from concourse.bass_utils import run_bass_kernel_spmd

    nc = bacc.Bacc("TRN2", target_bir_lowering=False, num_devices=1)
    arrays, args = {}, []
    for name in _INS:
        arrays[f"in_{name}"] = np.ascontiguousarray(inputs[name])
    for name, a in shape_constants().items():
        arrays[f"const_{name}"] = np.ascontiguousarray(a)
    for name, a in arrays.items():
        args.append(nc.dram_tensor(name, a.shape, mybir.dt.from_np(a.dtype), kind="ExternalInput").ap())
    args.append(nc.dram_tensor("out", (1, S, D), F32, kind="ExternalOutput").ap())
    attn_ffn_kernel(nc, *args)
    result = run_bass_kernel_spmd(nc, [arrays], core_ids=[0])
    return result.results[0]["out"]
```

```python
from contextlib import ExitStack

import numpy as np

import concourse.bass as bass
from concourse import mybir

F32 = mybir.dt.float32
F32R = mybir.dt.float32r
ALU = mybir.AluOpType
ACT = mybir.ActivationFunctionType
AX = mybir.AxisListType

P = 128
S, D = 1024, 512
H, KVH, HD = 32, 8, 128
E, R, O = 8, 16, 512
GROUP = H // KVH
NT, ND = S // P, D // P
CH = 512
TPC = CH // P
HALF = HD // 2
THETA = 10000.0
SCALE = 1.0 / float(np.sqrt(HD))
EPS = 1e-5
LORA_SCALING = 32 / 16
Q_START, Q_STOP = 34 + 72 + 1, S - 1
MASKED = -3.0e38
RING = 3

WINDOWS = [(0, 0), (0, 1), (1, 0), (1, 1)]
NW = len(WINDOWS)
BLOCKS = [TPC * (c + 1) for _, c in WINDOWS]
BLOCK0 = [sum(BLOCKS[:w]) for w in range(NW)]
BPH = sum(BLOCKS)
TILE_SLOTS = [[0, 0, 1, 1], [1, 2, 4, 6], [0, 0, 1, 1], [3, 4, 5, 6]]


def pieces_of(w, hh, more):
    next_group = more and hh == GROUP - 1
    if w == 0:
        return {0: ("LK", 0), 1: ("LK", 1), 2: ("OUT1", 0), 3: ("OUT1", 1)}
    if w == 1:
        return {0: ("LV", 0), 1: ("LV", 1), 3: ("LVT", 0), 5: ("LVT", 1), 6: ("OUT1", 2), 7: ("OUT1", 3)}
    if w == 2:
        ahead = {0: ("K", 0), 1: ("K", 1), 2: ("V", 0)} if next_group else {}
        return {**ahead, 3: ("Q", 0)} if more else {}
    ahead = {0: ("Q", 1)} if more else {}
    if next_group:
        ahead.update({1: ("V", 1), 2: ("VT", 0), 3: ("VT", 1)})
    slots = (4, 5, 6, 7) if hh == GROUP - 1 else (2, 4, 5, 7)
    return {**ahead, **{s: ("OUT0", n) for n, s in enumerate(slots)}}


ROPE = ("Q", "K", "LK")


def number_pieces():
    at, dve_at, n, m = {}, {}, 0, 0
    for hh in range(GROUP):
        for w in range(NW):
            for s, (name, _) in sorted(pieces_of(w, hh, True).items()):
                at[hh, w, s] = n
                n += 1
                if name not in ROPE:
                    dve_at[hh, w, s] = m
                    m += 1
    return at, n, dve_at, m


X_AT, XPG, FREE_AT, FREES_PER_GROUP = number_pieces()
X_BEFORE = 10
FREES_BEFORE = 6
ROPES_BEFORE = 4
ROPES_PER_GROUP = 2 * (2 * GROUP + 1)
VTS_PER_GROUP = 2 * (GROUP + 1)
LOADS_BEFORE = 6
LOADS_PER_GROUP = 5 * GROUP + 2

C_T, C_PV, C_B, C_OS, C_OL = 1, 3, 1, 1, 1


def p_offset(c, t):
    return P * sum(TPC * c + k + 1 for k in range(t))


def block_columns(c, j):
    return P * max(0, j - TPC * c)


def attn_ffn_kernel(nc, x_in, w_q, w_k, w_v, w_o, w_lq, w_lk, w_lv, w_out_latent, W, b, A, B, router_W, router_b,
                    cos_in, sin_in, mask_in, ident_in, pick_in, out):
    with ExitStack() as ctx:
        def sb(name, shape, dt=F32):
            return ctx.enter_context(nc.sbuf_tensor(name, shape, dt))

        def pair(name, shape):
            return sb(name + "_hi", shape, F32R), sb(name + "_lo", shape, F32R)

        def sem(name):
            return ctx.enter_context(nc.semaphore(name))

        cos = sb("cos", [P, S])
        sin = sb("sin", [P, S])
        mask = sb("mask", [P, S], mybir.dt.bfloat16)
        ident = sb("ident", [P, P])
        acc = sb("acc", [P, NT, D])
        xnT = pair("xnT", [P, ND, S])
        lqT = pair("lqT", [P, S])
        QT = pair("QT", [P, 2, S])
        KT = pair("KT", [P, S])
        LKT = pair("LKT", [P, S])
        V = pair("V", [P, NT, HD])
        LV = pair("LV", [P, NT, HD])
        vT = sb("vT", [P, S])
        probs = [sb(f"probs{c}", [P, p_offset(c, TPC)]) for c in range(2)]
        PT = pair("PT", [P, 2, CH])
        PTD = pair("PTD", [P, 2 * P])
        OT = pair("OT", [P, 2, S])
        o_raw = sb("o_raw", [P, 2, CH])
        inv_b = sb("inv_b", [P, CH])
        rot_half = sb("rot_half", [P, 2, CH])
        rot = sb("rot", [P, RING, CH])
        Wq = pair("Wq", [P, ND, HD])
        Wk = pair("Wk", [P, ND, HD])
        Wv = pair("Wv", [P, ND, HD])
        Wlv = pair("Wlv", [P, ND, HD])
        Wlk = pair("Wlk", [P, HD])
        Wo = pair("Wo", [P, D])
        Wlo = pair("Wlo", [P, D])
        stage = sb("stage", [P, 2, CH])
        nmax = sb("nmax", [P, 2, TPC])
        rsum = sb("rsum", [P, 2, TPC])
        rinv = sb("rinv", [P, 2, TPC])
        stats = inv_b[:, 64:64 + 6 * NT].rearrange("p (i n) -> p i n", n=6)
        mv = inv_b[:, 128:128 + 2 * NT].rearrange("p (i n) -> p i n", n=2)
        std = inv_b[:, 192:192 + 4 * NT].rearrange("p (n i) -> p n i", i=NT)

        scores = [ctx.enter_context(nc.psum_tensor(f"scores{i}", [P, 2, CH], F32)) for i in range(2)]
        bankT = [ctx.enter_context(nc.psum_tensor(f"bankT{i}", [P, CH], F32)) for i in range(2)]
        bankO = ctx.enter_context(nc.psum_tensor("bankO", [P, CH], F32))
        bankX = ctx.enter_context(nc.psum_tensor("bankX", [P, CH], F32))
        banksX = [bankX[:, :], scores[1][:, 1, :]]

        x_loaded, consts_loaded, w_loaded = sem("x_loaded"), sem("consts_loaded"), [sem("w_loaded0"), sem("w_loaded1")]
        ffn_loaded, out_stored = sem("ffn_loaded"), sem("out_stored")
        scored, transposed, pv_done, x_ready = sem("scored"), sem("transposed"), sem("pv_done"), sem("x_ready")
        row_maxed, pt_lo, x_free, o_scaled, inverted = (sem("row_maxed"), sem("pt_lo"), sem("x_free"),
                                                        sem("o_scaled"), sem("inverted"))
        dve_step, act_step = sem("dve_step"), sem("act_step")
        exped, pt_hi, b_copied, w_hi, rope_hi, o_hi, v_hi = (sem("exped"), sem("pt_hi"), sem("b_copied"), sem("w_hi"),
                                                             sem("rope_hi"), sem("o_hi"), sem("v_hi"))
        rope_raw, rope_half, rope_cos = sem("rope_raw"), sem("rope_half"), sem("rope_cos")
        rope_sum, rope_lo, o_lo, w_lo, cleared = (sem("rope_sum"), sem("rope_lo"), [sem("o_lo0"), sem("o_lo1")], sem("w_lo"),
                                                  sem("cleared"))
        xn_made, xt_ready, xt_hi, xt_lo = sem("xn_made"), sem("xt_ready"), sem("xt_hi"), sem("xt_lo")
        f_ready, f_hi, f_lo, f_free = sem("f_ready"), sem("f_hi"), sem("f_lo"), sem("f_free")
        y_done, f_chain, mask_made, score_seen = sem("y_done"), sem("f_chain"), sem("mask_made"), sem("score_seen")

        f32 = lambda ap: ap.bitcast(F32)

        def block_no(g, hh, w, j):
            return (g * GROUP + hh) * BPH + BLOCK0[w] + j

        def unit_no(g, hh, w):
            return (g * GROUP + hh) * NW + w

        def n_out_low(g, hh, kind):
            return (g * GROUP + hh) * 2 + kind + 1 + C_OL

        def n_transposed(g, hh, w, j):
            return block_no(g, hh, w, j) + unit_no(g, hh, w) + 1 + C_T

        def n_piece(g, hh, w, s):
            skipped = 8 if isinstance(g, int) and g == KVH - 1 and (hh, w) == (GROUP - 1, NW - 1) else 0
            return g * XPG + (X_BEFORE + X_AT[hh, w, s] + 1 - skipped)

        def n_free(g, hh, w, s):
            skipped = 4 if isinstance(g, int) and g == KVH - 1 and (hh, w) == (GROUP - 1, NW - 1) else 0
            return g * FREES_PER_GROUP + (FREES_BEFORE + FREE_AT[hh, w, s] + 1 - skipped)

        def piece_bank(hh, w, s, more):
            return sorted(pieces_of(w, hh, more)).index(s) % 2 if w in (1, 3) else 0

        def bank_x_taken(eng, g, hh, w, s, last):
            bank = piece_bank(hh, w, s, not (last and hh == GROUP - 1))
            ahead = [(h2, w2, s2, name) for h2, w2, more in windows(g, last) for s2, name in
                     sorted(pieces_of(w2, h2, more).items())
                     if (h2, w2, s2) < (hh, w, s) and piece_bank(h2, w2, s2, more) == bank]
            if bank and not (ahead and ahead[-1][:2] == (hh, w)):
                eng.wait_ge(row_maxed, tiles_made(g, hh, w))
                return
            if not ahead:
                eng.wait_ge(x_free, g * FREES_PER_GROUP + FREES_BEFORE)
                return
            h2, w2, s2, (name, n) = ahead[-1]
            if name in ROPE:
                eng.wait_ge(rope_raw, rope_no(g, h2, name, n) + 1)
            else:
                eng.wait_ge(x_free, n_free(g, h2, w2, s2))

        def rope_no(g, hh, name, n):
            base = g * ROPES_PER_GROUP + (ROPES_BEFORE + 4 * hh)
            return base + {"LK": 0, "K": 2, "Q": 4 if hh == GROUP - 1 else 2}[name] + n

        def vt_no(g, hh, name, n):
            return g * VTS_PER_GROUP + (2 + 2 * hh + {"LVT": 0, "VT": 2}[name] + n)

        def load_no(g, hh, name):
            order = (["Wk", "Wv"] if hh == GROUP - 1 else []) + ["Wq", "Wo", "Wlo", "Wlk", "Wlv"]
            return g * LOADS_PER_GROUP + (LOADS_BEFORE + 5 * hh + order.index(name))

        def n_latent_load(g, hh, name):
            before = g * LOADS_PER_GROUP + (LOADS_BEFORE + 5 * hh)
            return before - (1 if name == "Wlk" else 0)

        def tiles_made(g, hh, w):
            return TPC * (unit_no(g, hh, w) + 1)

        def last_block(g, hh, w):
            return block_no(g, hh, w, BLOCKS[w] - 1)

        def windows(g, last):
            for hh in range(GROUP):
                for w in range(NW):
                    yield hh, w, not (last and hh == GROUP - 1)

        def ring_slot(hh, w, j):
            ahead = sum(BLOCKS[k] - 1 for k in range(w)) + j
            return None if j == BLOCKS[w] - 1 else ahead % 2

        def pt_place(half, hh, w, j):
            slot = ring_slot(hh, w, j)
            if slot is None:
                return PTD[half][:, P:2 * P]
            return PT[half][:, slot, block_columns(WINDOWS[w][1], j):CH]

        def bank_no(hh, w, j):
            return (hh * (BPH + NW) + BLOCK0[w] + w + j) % 2

        def tile_view(ap, c):
            return ap if c == 0 else ap.rearrange("p (a n) -> p a n", a=2)

        def tile_bank(n, c, width):
            return scores[n % 2][:, 0, 0:width] if c == 0 else scores[n % 2][:, :, 0:width // 2]

        def prob_tile(c, t):
            width = P * (TPC * c + t + 1)
            return probs[c][:, p_offset(c, t):p_offset(c, t) + width]

        block = ctx.enter_context(nc.Block())

        @block.sync
        def _(sp):
            sp.dma_start(acc[:, :, :], x_in[0].rearrange("(i p) d -> p i d", p=P)).then_inc(x_loaded, 16)
            for place, src in ((ident, ident_in), (cos, cos_in), (sin, sin_in), (vT, mask_in)):
                sp.dma_start(place[:, :], src).then_inc(consts_loaded, 16)

            def load(no, slot, src):
                if not (isinstance(no, int) and no < 2):
                    sp.wait_ge(w_lo, no - 1)
                width = CH if len(src.shape) == 3 or src.shape[1] == CH else HD
                place = stage[:, slot, 0:width]
                if len(src.shape) == 3:
                    place = place.rearrange("p (k n) -> p k n", k=ND)
                sp.dma_start(place, src).then_inc(w_loaded[slot], 16)

            def columns(w, at):
                return w[:, bass.ds(at, HD)].rearrange("(k p) n -> p k n", p=P)

            for no, src in enumerate((columns(w_lq, 0), columns(w_q, 0), columns(w_k, 0), columns(w_v, 0),
                                      w_lk[:, 0:HD], columns(w_lv, 0))):
                load(no, no % 2, src)

            def group_of_heads(g, last):
                for hh in range(GROUP):
                    more = not (last and hh == GROUP - 1)
                    here = (g * GROUP + hh) * HD
                    after = (g * GROUP + hh + 1) * HD

                    def fetch(name, src):
                        no = load_no(g, hh, name)
                        load(no, load_no(0, hh, name) % 2, src)

                    if more:
                        if hh == GROUP - 1:
                            fetch("Wk", columns(w_k, (g + 1) * HD))
                            fetch("Wv", columns(w_v, (g + 1) * HD))
                        fetch("Wq", columns(w_q, after))
                    if not more:
                        for k, src in enumerate((w_o[bass.ds(here, HD), :], w_out_latent[bass.ds(here, HD), :])):
                            load(load_no(g, hh, "Wk") + k, (load_no(0, hh, "Wk") + k) % 2, src)
                        continue
                    fetch("Wo", w_o[bass.ds(here, HD), :])
                    fetch("Wlo", w_out_latent[bass.ds(here, HD), :])
                    fetch("Wlk", w_lk[:, bass.ds(after, HD)])
                    fetch("Wlv", columns(w_lv, after))

            with sp.Fori(0, KVH - 1) as g:
                group_of_heads(g, False)
            group_of_heads(KVH - 1, True)

            sp.wait_ge(x_ready, n_piece(KVH - 1, GROUP - 1, 1, 7))
            sp.wait_ge(transposed, n_transposed(KVH - 1, GROUP - 1, 3, BLOCKS[3] - 1))
            w_raw = probs[1][:, 0:ND * D].rearrange("p (k n) -> p k n", k=ND)
            sp.dma_start(w_raw, W.rearrange("(k p) n -> p k n", p=P)).then_inc(ffn_loaded, 16)
            sp.dma_start(probs[1][:, ND * D:ND * D + D], A.rearrange("e r d -> (e r) d")).then_inc(ffn_loaded, 16)
            b_raw = probs[1][:, ND * D + D:ND * D + 2 * D].rearrange("p (k e r) -> p k e r", k=ND, e=E)
            for k in range(ND):
                sp.dma_start(b_raw[:, k], B[:, k * P:(k + 1) * P, :].rearrange("e p r -> p e r"))\
                    .then_inc(ffn_loaded, 16)
            sp.dma_start(probs[0][0:E, 0:D], router_W).then_inc(ffn_loaded, 16)
            sp.dma_start(probs[0][:, D:2 * D], b.rearrange("(a n) -> a n", a=1).broadcast_to([P, D]))\
                .then_inc(ffn_loaded, 16)
            sp.dma_start(probs[0][:, 2 * D:2 * D + E],
                         router_b.rearrange("(a n) -> a n", a=1).broadcast_to([P, E])).then_inc(ffn_loaded, 16)
            sp.dma_start(probs[0][:, 2 * D + E:2 * D + 2 * E], pick_in).then_inc(ffn_loaded, 16)
            for i in range(NT):
                sp.wait_ge(y_done, i + 1)
                sp.dma_start(out[0, i * P:(i + 1) * P, :], acc[:, i, :]).then_inc(out_stored, 16)
            sp.wait_ge(out_stored, 16 * NT)

        n_ffn_loads = 6 + ND
        W_raw = probs[1][:, 0:ND * D].rearrange("p (k n) -> p k n", k=ND)
        A_raw = probs[1][:, ND * D:ND * D + D]
        B_raw = probs[1][:, ND * D + D:ND * D + 2 * D].rearrange("p (k c) -> p k c", k=ND)
        rw_raw = probs[0][0:E, 0:D]
        bias = probs[0][:, D:2 * D]
        r_bias = probs[0][:, 2 * D:2 * D + E]
        pick = probs[0][:, 2 * D + E:2 * D + 2 * E]
        WT = [h[:, :, :].rearrange("p a b -> p (a b)").rearrange("p (k n) -> p k n", k=ND) for h in OT]
        AT = [h[:, 0:CH].rearrange("p (k n) -> p k n", k=ND) for h in LKT]
        BT = [h[:, 0:O] for h in KT]
        rwT = inv_b[:, 0:ND * E].rearrange("p (k e) -> p k e", k=ND)
        tT = lqT
        xsum = rot_half[:, 0, 0:ND]
        soft = rot_half[:, 0, 64:64 + 8 * E].rearrange("p (k e) -> p k e", e=E)

        @block.tensor
        def _(pe):
            def mm3(place, left, right, start, stop):
                pe.matmul(place, left[1], right[0], start=start, stop=False)
                pe.matmul(place, left[0], right[1], start=False, stop=False)
                return pe.matmul(place, left[0], right[0], start=False, stop=stop)

            def both(pair_, *index):
                return [h[index] for h in pair_]

            ALL = slice(None)

            def normalised_transposes(made, ready):
                for i in range(NT):
                    pe.wait_ge(xn_made, made + i + 1)
                    if i >= 2 or made:
                        pe.wait_ge(xt_lo, made + i - 1)
                    for k in range(ND):
                        mm = pe.transpose(bankT[i % 2][:, k * P:(k + 1) * P],
                                          o_raw[:, i % 2, k * P:(k + 1) * P], ident[:, :])
                    mm.then_inc(ready, 1)

            def project(weights, n, bank=0):
                for k in range(ND):
                    mm = mm3(banksX[bank], both(weights, ALL, k, ALL), both(xnT, ALL, k, slice(n * CH, n * CH + CH)),
                             k == 0, k == ND - 1)
                return mm

            def value_transposes(n, bank=0):
                for i in range(TPC):
                    mm = pe.transpose(banksX[bank][:, i * P:(i + 1) * P],
                                      vT[:, (n * TPC + i) * P:(n * TPC + i + 1) * P], ident[:, :])
                return mm

            def out_tile(c, i, bank=0):
                rows = slice((TPC * c + i) * P, (TPC * c + i + 1) * P)
                mm3(banksX[bank], both(OT, ALL, 0, rows), both(Wo, ALL, ALL), True, False)
                return mm3(banksX[bank], both(OT, ALL, 1, rows), both(Wlo, ALL, ALL), False, True)

            def score_tile(no, parity, head, kind, c, t):
                if not (isinstance(no, int) and no < 2):
                    pe.wait_ge(row_maxed, no - 1)
                i = TPC * c + t
                width = (i + 1) * P
                keys = LKT if kind else KT
                query = both(QT, ALL, head % 2, slice(i * P, (i + 1) * P))
                if c == 0:
                    n = max(width, 2 * P)
                    mm = mm3(scores[parity][:, 0, 0:n], query, both(keys, ALL, slice(0, n)), True, True)
                else:
                    for a in range(2):
                        part = slice(a * width // 2, (a + 1) * width // 2)
                        mm = mm3(scores[parity][:, a, 0:width // 2], query, both(keys, ALL, part), True, True)
                mm.then_inc(scored, 1)

            def transpose_block(g, hh, w, j):
                c = WINDOWS[w][1]
                no = block_no(g, hh, w, j)
                if j == 0:
                    pe.wait_ge(exped, tiles_made(g, hh, w))
                if j == 1:
                    pe.wait_ge(b_copied, unit_no(g, hh, w) + C_B)
                elif not (isinstance(no, int) and no == 0):
                    pe.wait_ge(pt_lo, no if j == 0 else no - 1)
                for t in range(max(0, j - TPC * c), TPC):
                    at = p_offset(c, t) + j * P
                    mm = pe.transpose(bankT[bank_no(hh, w, j)][:, t * P:(t + 1) * P],
                                      probs[c][:, at:at + P], ident[:, :])
                mm.then_inc(transposed, 1)

            def transpose_sums(g, hh, w):
                c = WINDOWS[w][1]
                pe.wait_ge(inverted, unit_no(g, hh, w) + 1)
                pe.wait_ge(pt_lo, last_block(g, hh, w))
                for t in range(TPC):
                    mm = pe.transpose(bankT[bank_no(hh, w, BLOCKS[w])][:, t * P:(t + 1) * P],
                                      rinv[:, c, t:t + 1].broadcast_to([P, P]), ident[:, :])
                mm.then_inc(transposed, 1)

            def pv_block(g, hh, w, j):
                kind, c = WINDOWS[w]
                no = block_no(g, hh, w, j)
                pe.wait_ge(pt_lo, no + 1)
                if j == 0:
                    pe.wait_ge(o_scaled, unit_no(g, hh, w) + C_OS)
                values = both(LV if kind else V, ALL, j, ALL)
                if j == BLOCKS[w] - 1:
                    mm = mm3(bankO[:, CH - 2 * P:CH], values, both(PTD, ALL, ALL), False, True)
                else:
                    at = block_columns(c, j)
                    mm = mm3(bankO[:, at:CH], values, both(PT, ALL, ring_slot(hh, w, j), slice(at, CH)), j == 0, False)
                mm.then_inc(pv_done, 1)

            def piece(g, hh, w, s, name, n):
                bank_x_taken(pe, g, hh, w, s, g_last[0])
                bank = piece_bank(hh, w, s, not (g_last[0] and hh == GROUP - 1))
                if name == "LK":
                    pe.wait_ge(w_lo, n_latent_load(g, hh, "Wlk"))
                    mm = mm3(bankX[:, :], both(Wlk, ALL, ALL), both(lqT, ALL, slice(n * CH, n * CH + CH)), True, True)
                elif name == "LV":
                    pe.wait_ge(w_lo, n_latent_load(g, hh, "Wlv"))
                    mm = project(Wlv, n, bank)
                elif name in ("LVT", "VT"):
                    mm = value_transposes(n, bank)
                elif name == "Q":
                    pe.wait_ge(w_lo, load_no(g, hh, "Wq") + 1)
                    mm = project(Wq, n, bank)
                elif name == "K":
                    pe.wait_ge(w_lo, load_no(g, hh, "Wk") + 1)
                    mm = project(Wk, n, bank)
                elif name == "V":
                    pe.wait_ge(w_lo, load_no(g, hh, "Wv") + 1)
                    mm = project(Wv, n, bank)
                elif name == "OUT0":
                    pe.wait_ge(w_lo, out_weights(g, hh, g_last[0]))
                    pe.wait_ge(o_lo[0], n_out_low(g, hh, 1))
                    mm = out_tile(0, n, bank)
                else:
                    pe.wait_ge(o_lo[1], n_out_low(g, hh, 0) - 1)
                    mm = out_tile(1, n, bank)
                mm.then_inc(x_ready, 1)

            g_last = [False]

            def out_weights(g, hh, last):
                if last and hh == GROUP - 1:
                    return load_no(g, hh, "Wk") + 2
                return load_no(g, hh, "Wlo") + 1

            def group_of_heads(g, last):
                g_last[0] = last
                for hh, w, more in windows(g, last):
                    nw, nhh = (w + 1) % NW, hh + (w == NW - 1)
                    for s in range(BLOCKS[w]):
                        if more or w < NW - 1:
                            for t in range(TPC):
                                if TILE_SLOTS[w][t] != s:
                                    continue
                                no = tiles_made(g, hh, w) + t
                                if t == 0 and w in (1, 2):
                                    pe.wait_ge(rope_lo, rope_no(g, hh, "LK", w - 1) + 1)
                                if t == 0 and w == 3:
                                    pe.wait_ge(rope_lo, rope_no(g, hh, "Q", 0) + 1)
                                if t == 0 and w == 0:
                                    pe.wait_ge(rope_lo, rope_no(g, hh, "LK", 0))
                                if t == 1 and w == 0:
                                    pe.wait_ge(x_free, g * FREES_PER_GROUP + FREES_BEFORE if hh == 0 else
                                               n_free(g, hh - 1, 3, 7))
                                if t == 1 and w == 2:
                                    pe.wait_ge(x_free, n_free(g, hh, 1, 7))
                                score_tile(no, t % 2, nhh, WINDOWS[nw][0], WINDOWS[nw][1], t)
                        if s in pieces_of(w, hh, more):
                            piece(g, hh, w, s, *pieces_of(w, hh, more)[s])
                        if s + 2 < BLOCKS[w]:
                            transpose_block(g, hh, w, s + 2)
                        elif s + 2 == BLOCKS[w]:
                            transpose_sums(g, hh, w)
                        if s == 0 and w in (0, 2):
                            if w == 2:
                                pe.wait_ge(x_free, n_free(g, hh, 1, 5))
                            elif hh == 0:
                                pe.wait_ge(x_free, g * FREES_PER_GROUP + FREES_BEFORE)
                        pv_block(g, hh, w, s)
                    for j in range(2):
                        if nhh < GROUP:
                            transpose_block(g, nhh, nw, j)
                        elif more:
                            transpose_block(g + 1, 0, 0, j)

            pe.sem_inc(transposed, C_T)
            pe.sem_inc(pv_done, C_PV)
            pe.wait_ge(consts_loaded, 64)
            normalised_transposes(0, xt_ready)
            pe.wait_ge(xt_lo, NT)
            for x, (weights, n) in enumerate([(Wlv, 0), (Wlv, 1), (Wq, 0), (Wq, 1), (Wk, 0), (Wk, 1), (Wv, 0), (Wv, 1)]):
                pe.wait_ge(w_lo, x // 2 + 1)
                if 3 <= x <= 6:
                    pe.wait_ge(rope_raw, x - 2)
                elif x:
                    pe.wait_ge(x_free, x if x < 3 else 3)
                project(weights, n).then_inc(x_ready, 1)
            for n in range(2):
                pe.wait_ge(x_free, 4 + n)
                value_transposes(n).then_inc(x_ready, 1)
            pe.wait_ge(rope_lo, ROPES_BEFORE)
            for t in range(TPC):
                score_tile(t, t % 2, 0, 0, 0, t)
            transpose_block(0, 0, 0, 0)
            transpose_block(0, 0, 0, 1)

            with pe.Fori(0, KVH - 1) as g:
                group_of_heads(g, False)
            group_of_heads(KVH - 1, True)

            for n in range(TPC):
                pe.wait_ge(x_free, n_free(KVH - 1, GROUP - 1, 3, 7) + n)
                if n == 0:
                    pe.wait_ge(o_lo[1], 2 * H + C_OL)
                out_tile(1, n).then_inc(x_ready, 1)

            pe.wait_ge(ffn_loaded, 16 * n_ffn_loads)
            jobs = []
            for k in range(ND):
                jobs.append([(bankT, m, W_raw[:, m, k * P:(k + 1) * P]) for m in range(ND)])
            jobs.append([(bankT, k, A_raw[:, k * P:(k + 1) * P]) for k in range(ND)])
            jobs.append([(bankT, k, B_raw[:, k, :]) for k in range(ND)])
            pe.wait_ge(b_copied, H * NW + C_B)
            pe.wait_ge(pt_lo, H * BPH)
            for n, job in enumerate(jobs):
                if n >= 2:
                    pe.wait_ge(f_lo, n - 1)
                for banks, m, src in job:
                    mm = pe.transpose(banks[n % 2][:, m * P:(m + 1) * P], src, ident[:, :])
                mm.then_inc(f_ready, 1)
            pe.wait_ge(f_lo, len(jobs) - 1)
            for k in range(ND):
                mm = pe.transpose(bankT[0][:, k * E:(k + 1) * E], rw_raw[:, k * P:(k + 1) * P], ident[0:E, 0:E])
            mm.then_inc(f_ready, 1)
            pe.wait_ge(f_lo, len(jobs) + 1)
            normalised_transposes(NT, xt_ready)
            pe.wait_ge(xt_lo, 2 * NT)
            for n in range(2):
                for k in range(ND):
                    mm = mm3(scores[0][:, n, :], both(AT, ALL, k, ALL),
                             both(xnT, ALL, k, slice(n * CH, n * CH + CH)), k == 0, k == ND - 1)
                mm.then_inc(f_ready, 1)
            pe.wait_ge(f_lo, len(jobs) + 2)
            for k in range(ND):
                mm = pe.matmul(bankO[:, 0:E], xsum[:, k:k + 1].broadcast_to([P, P]), rwT[:, k, :],
                               start=(k == 0), stop=(k == ND - 1))
            mm.then_inc(f_ready, 1)
            pe.wait_ge(f_lo, len(jobs) + 4)
            for i in range(NT):
                place = scores[1][:, i % 2, :]
                if i >= 2:
                    pe.wait_ge(y_done, i - 1)
                rows = slice(i * P, (i + 1) * P)
                for k in range(ND):
                    mm3(place, both(xnT, ALL, k, rows), both(WT, ALL, k, ALL), k == 0, False)
                mm3(place, both(tT, ALL, rows), BT, False, True).then_inc(f_ready, 1)

        @block.scalar
        def _(act):
            def copy(place, src):
                return act.activation(place, src, ACT.Copy)

            def root(step):
                act.wait_ge(dve_step, step)
                act.activation(std[:, 1, :], std[:, 0, :], ACT.Sqrt).then_inc(act_step, 1)

            def normalised_hi(made):
                for i in range(NT):
                    act.wait_ge(xt_ready, made + i + 1)
                    copy(xnT[0][:, :, i * P:(i + 1) * P], bankT[i % 2][:, :].rearrange("p (k n) -> p k n", k=ND))\
                        .then_inc(xt_hi, 1)

            def weights_hi(no, slot, per_slot, places):
                act.wait_ge(w_loaded[slot], 16 * per_slot)
                place = places[0]
                src = stage[:, slot, 0:HD if places is Wlk else CH]
                if len(place.shape) == 3:
                    copy(place[:, :, :], src.rearrange("p (k n) -> p k n", k=ND)).then_inc(w_hi, 1)
                else:
                    copy(place[:, :], src).then_inc(w_hi, 1)

            def fetched(g, hh, name, places, at=None):
                no = load_no(0, hh, name) if at is None else at
                weights_hi(None, no % 2, g * (LOADS_PER_GROUP // 2) + (no // 2 + 1), places)

            def rope_take(n_x, no, slot, bank=0):
                if not (isinstance(no, int) and no < RING):
                    act.wait_ge(rope_lo, no - (RING - 1))
                act.wait_ge(x_ready, n_x)
                copy(rot[:, slot, :], banksX[bank]).then_inc(rope_raw, 1)

            def rope_high(no, slot, place):
                act.wait_ge(rope_sum, no + 1)
                copy(place, rot[:, slot, :]).then_inc(rope_hi, 1)

            def value_high(n_x, place, n, bank=0):
                act.wait_ge(x_ready, n_x)
                copy(place[:, n * TPC:(n + 1) * TPC, :], banksX[bank].rearrange("p (k n) -> p k n", k=TPC))\
                    .then_inc(v_hi, 1)

            def exp_tile(no, c, t):
                act.wait_ge(row_maxed, no + 1)
                act.activation(prob_tile(c, t), prob_tile(c, t), ACT.Exp, bias=nmax[:, c, t:t + 1], scale=-1.0,
                               accum_out=rsum[:, c, t:t + 1]).then_inc(exped, 1)

            def block_hi(g, hh, w, j):
                no = block_no(g, hh, w, j)
                c = WINDOWS[w][1]
                if not (isinstance(no, int) and no == 0):
                    ahead = 2 if (j < 2 or j == BLOCKS[w] - 1) else 1
                    act.wait_ge(pv_done, no - ahead + C_PV)
                else:
                    act.wait_ge(cleared, 1)
                act.wait_ge(transposed, n_transposed(g, hh, w, j))
                copy(pt_place(0, hh, w, j), bankT[bank_no(hh, w, j)][:, block_columns(c, j):CH]).then_inc(pt_hi, 1)

            def sums_copy(g, hh, w):
                act.wait_ge(o_scaled, unit_no(g, hh, w) + C_OS)
                act.wait_ge(transposed, n_transposed(g, hh, w, BLOCKS[w]))
                copy(inv_b[:, :], bankT[bank_no(hh, w, BLOCKS[w])][:, :]).then_inc(b_copied, 1)

            highs = [{(0, 3): ("LK", 0), (1, 0): ("LK", 1), (3, 1): ("Q", 0), (3, 3): ("Q", 1)} for _ in range(GROUP)]
            highs[GROUP - 1].update({(2, 3): ("K", 0), (3, 0): ("K", 1)})

            def group_of_heads(g, last):
                for hh, w, more in windows(g, last):
                    nw, nhh = (w + 1) % NW, hh + (w == NW - 1)
                    kind, c = WINDOWS[w]
                    third = last and hh == GROUP - 1
                    for s in range(BLOCKS[w]):
                        name, n = pieces_of(w, hh, more).get(s, ("", 0))
                        if name == "LK":
                            rope_take(n_piece(g, hh, w, s), rope_no(g, hh, name, n), rope_no(0, hh, name, n) % RING,
                                      piece_bank(hh, w, s, more))
                        if name == "LK":
                            block_hi(g, hh, w, s + 2)
                        if more or w < NW - 1:
                            for t in range(TPC):
                                if TILE_SLOTS[w][t] == s:
                                    exp_tile(tiles_made(g, hh, w) + t, WINDOWS[nw][1], t)
                        if name in ("Q", "K"):
                            rope_take(n_piece(g, hh, w, s), rope_no(g, hh, name, n), rope_no(0, hh, name, n) % RING,
                                      piece_bank(hh, w, s, more))
                        if w == 1 and s in (3, 5):
                            if s == 3:
                                act.wait_ge(pv_done, last_block(g, hh, 0) + 1 + C_PV)
                            value_high(n_piece(g, hh, 1, s), LV[0], s // 5, piece_bank(hh, 1, s, more))
                        if w == 3 and s in (2, 3) and more and hh == GROUP - 1:
                            if s == 2:
                                act.wait_ge(pv_done, last_block(g, hh, 1) + 1 + C_PV)
                            value_high(n_piece(g, hh, 3, s), V[0], s - 2, piece_bank(hh, 3, s, more))
                        if s + 2 < BLOCKS[w] and name != "LK":
                            block_hi(g, hh, w, s + 2)
                        elif s + 2 == BLOCKS[w]:
                            sums_copy(g, hh, w)
                        if (w, s) in highs[hh]:
                            name, n = highs[hh][w, s]
                            if (w, s) in ((0, 3), (2, 3), (3, 1)):
                                act.wait_ge(scored, tiles_made(g, hh, w))
                            if more or name == "LK":
                                place = {"LK": LKT[0][:, n * CH:(n + 1) * CH],
                                         "K": KT[0][:, n * CH:(n + 1) * CH],
                                         "Q": QT[0][:, (hh + 1) % 2, n * CH:(n + 1) * CH]}[name]
                                rope_high(rope_no(g, hh, name, n), rope_no(0, hh, name, n) % RING, place)
                        if w == 0 and s >= 2 and more and hh == GROUP - 1:
                            fetched(g, hh, *(("Wk", Wk), ("Wv", Wv))[s - 2])
                        if w == 1 and s == 1 and more:
                            act.wait_ge(x_ready, n_piece(g, hh, 1, 0))
                            fetched(g, hh, "Wq", Wq)
                        if w == 2 and s < 2:
                            if s == 0:
                                act.wait_ge(x_ready, n_piece(g, hh, 1, 7))
                            name, places = (("Wo", Wo), ("Wlo", Wlo))[s]
                            fetched(g, hh, name, places, load_no(0, hh, "Wk") + s if third else None)
                        if w == 3 and s in (5, 6) and more:
                            name, places = (("Wlk", Wlk), ("Wlv", Wlv))[s - 5]
                            fetched(g, hh, name, places)
                    for j in range(2):
                        if nhh < GROUP:
                            block_hi(g, nhh, nw, j)
                        elif more:
                            block_hi(g + 1, 0, 0, j)
                    act.wait_ge(x_ready, n_piece(g, hh, *((0, 0) if c == 0 else (1, 7))))
                    act.wait_ge(o_scaled, unit_no(g, hh, w) + 1 + C_OS)
                    copy(OT[0][:, kind, c * CH:(c + 1) * CH], o_raw[:, w % 2, :]).then_inc(o_hi, 1)

            act.sem_inc(b_copied, C_B)
            root(1)
            normalised_hi(0)
            for no, places in enumerate((Wlv, Wq, Wk, Wv)):
                weights_hi(no, no % 2, no // 2 + 1, places)
            for n in range(2):
                act.wait_ge(x_ready, n + 1)
                copy(lqT[0][:, n * CH:(n + 1) * CH], bankX[:, :]).then_inc(v_hi, 1)
            weights_hi(4, 0, 3, Wlk)
            weights_hi(5, 1, 3, Wlv)
            for p in range(ROPES_BEFORE):
                n = p % 2
                rope_take(3 + p, p, p % RING)
                rope_high(p, p % RING, (QT[0][:, 0, n * CH:(n + 1) * CH], KT[0][:, n * CH:(n + 1) * CH])[p // 2])
            for n in range(2):
                value_high(9 + n, V[0], n)
            for t in range(TPC):
                exp_tile(t, 0, t)
            block_hi(0, 0, 0, 0)
            block_hi(0, 0, 0, 1)

            with act.Fori(0, KVH - 1) as g:
                group_of_heads(g, False)
            group_of_heads(KVH - 1, True)

            for n in range(ND + 2):
                act.wait_ge(f_ready, n + 1)
                if n == 0:
                    act.wait_ge(x_ready, n_piece(KVH - 1, GROUP - 1, 3, 7) + TPC)
                src = bankT[n % 2][:, :]
                if n < ND:
                    copy(WT[0][:, n, :], src).then_inc(f_hi, 1)
                elif n == ND:
                    copy(AT[0], src.rearrange("p (k n) -> p k n", k=ND)).then_inc(f_hi, 1)
                else:
                    copy(BT[0], src).then_inc(f_hi, 1)
            root(3)
            normalised_hi(NT)
            act.wait_ge(f_free, 1)
            act.activation(soft[:, 2, :], soft[:, 0, :], ACT.Exp, bias=soft[:, 1, 0:1], scale=1.0,
                           accum_out=soft[:, 1, 1:2]).then_inc(act_step, 1)
            for n in range(2):
                act.wait_ge(f_free, 2 + n)
                copy(tT[0][:, n * CH:(n + 1) * CH], o_raw[:, n, :]).then_inc(f_hi, 1)

        @block.vector
        def _(dve):
            def statistics(step):
                if step:
                    dve.wait_ge(y_free_sem, y_free_count)
                for i in range(NT):
                    dve.bn_stats(stats[:, i, :], acc[:, i, :]).then_inc(dve_chain, 1)
                chain[0] += NT
                dve.wait_ge(dve_chain, chain[0])
                for i in range(NT):
                    dve.bn_aggr(mv[:, i, :], stats[:, i, :]).then_inc(dve_chain, 1)
                chain[0] += NT
                dve.wait_ge(dve_chain, chain[0])
                dve.tensor_scalar(std[:, 0, :], mv[:, :, 1], EPS, None, ALU.add).then_inc(dve_step, 1)
                dve.wait_ge(act_step, step // 2 + 1)
                link(dve.reciprocal(std[:, 2, :], std[:, 1, :]))
                link(dve.tensor_tensor(std[:, 3, :], std[:, 2, :], std[:, 0, :], ALU.mult))
                link(dve.tensor_tensor(std[:, 2, :], std[:, 3, :], std[:, 1, :], ALU.add))
                link(dve.tensor_scalar(std[:, 3, :], std[:, 2, :], 0.5, None, ALU.mult))
                dve.reciprocal(std[:, 2, :], std[:, 3, :]).then_inc(dve_step, 1)
                dve.wait_ge(dve_step, step + 2)

            chain = [0]
            dve_chain = f_chain
            y_free_sem, y_free_count = x_free, n_free(KVH - 1, GROUP - 1, 3, 7) + TPC

            def link(ins):
                chain[0] += 1
                ins.then_inc(dve_chain, 1)
                dve.wait_ge(dve_chain, chain[0])

            def normalise(made):
                for i in range(NT + 1):
                    if i < NT:
                        if i >= 2:
                            dve.wait_ge(xt_ready, made + i - 1)
                        dve.tensor_scalar(o_raw[:, i % 2, :], acc[:, i, :], mv[:, i, 0:1], std[:, 2, i:i + 1],
                                          ALU.subtract, ALU.mult).then_inc(xn_made, 1)
                    if i:
                        j = i - 1
                        dve.wait_ge(xt_hi, made + j + 1)
                        rows = slice(j * P, (j + 1) * P)
                        dve.tensor_tensor(xnT[1][:, :, rows], bankT[j % 2][:, :].rearrange("p (k n) -> p k n", k=ND),
                                          f32(xnT[0][:, :, rows]), ALU.subtract).then_inc(xt_lo, 1)

            def row_max(no, parity, c, t):
                dve.wait_ge(scored, no + 1)
                dve.sem_inc(score_seen, 1)
                width = P * (TPC * c + t + 1)
                place = tile_view(prob_tile(c, t), c)
                src = scores[parity][:, 0, 0:width] if c == 0 else scores[parity][:, :, 0:width // 2]
                dve.tensor_tensor_reduce(place, src, tile_view(mask[:, S - width:S], c), -SCALE, -MASKED,
                                         ALU.add, ALU.min, nmax[:, c, t:t + 1]).then_inc(row_maxed, 1)

            def block_lo(g, hh, w, j):
                c = WINDOWS[w][1]
                dve.wait_ge(pt_hi, block_no(g, hh, w, j) + 1)
                dve.tensor_tensor(pt_place(1, hh, w, j), bankT[bank_no(hh, w, j)][:, block_columns(c, j):CH],
                                  f32(pt_place(0, hh, w, j)), ALU.subtract).then_inc(pt_lo, 1)

            def rotate(no, slot, n):
                if not (isinstance(no, int) and no < 2):
                    dve.wait_ge(rope_sum, no - 1)
                dve.wait_ge(rope_raw, no + 1)
                t = slice(n * CH, (n + 1) * CH)
                dve.tensor_tensor(rot_half[0:HALF, n, :], rot[HALF:HD, slot, :], sin[HALF:HD, t], ALU.mult)
                dve.tensor_tensor(rot_half[HALF:HD, n, :], rot[0:HALF, slot, :], sin[0:HALF, t], ALU.mult)\
                    .then_inc(rope_half, 1)

            def value_copy(n_x, n, bank=0):
                dve.wait_ge(x_ready, n_x)
                dve.tensor_copy(vT[:, n * CH:(n + 1) * CH], banksX[bank]).then_inc(x_free, 1)

            def value_lo(n_v, places, n, bank=0):
                dve.wait_ge(v_hi, n_v)
                rows = slice(n * TPC, (n + 1) * TPC)
                dve.tensor_tensor(places[1][:, rows, :], banksX[bank].rearrange("p (k n) -> p k n", k=TPC),
                                  f32(places[0][:, rows, :]), ALU.subtract).then_inc(x_free, 1)

            def add_out(n_x, n_taken, i, bank=0):
                dve.wait_ge(x_ready, n_x)
                dve.wait_ge(x_free, n_taken - 1)
                dve.tensor_tensor(acc[:, i, :], banksX[bank], acc[:, i, :], ALU.add).then_inc(x_free, 1)

            def piece(g, hh, w, s, name, n, bank):
                n_x = n_piece(g, hh, w, s)
                if name in ROPE:
                    rotate(rope_no(g, hh, name, n), rope_no(0, hh, name, n) % RING, n)
                elif name in ("V", "LV"):
                    value_copy(n_x, n, bank)
                elif name in ("VT", "LVT"):
                    value_lo(vt_no(g, hh, name, n) + 3, V if name == "VT" else LV, n, bank)
                else:
                    add_out(n_x, n_free(g, hh, w, s), n + (TPC if name == "OUT1" else 0), bank)

            def scale_out(g, hh, w):
                unit = unit_no(g, hh, w)
                kind, c = WINDOWS[w]
                dve.wait_ge(o_lo[c], n_out_low(g, hh, kind) - 1)
                dve.wait_ge(pv_done, last_block(g, hh, w) + 1 + C_PV)
                dve.wait_ge(b_copied, unit + 1 + C_B)
                dve.tensor_tensor(o_raw[:, w % 2, :], bankO[:, :], inv_b[:, :], ALU.mult).then_inc(o_scaled, 1)

            def out_low(g, hh, w):
                kind, c = WINDOWS[w]
                dve.wait_ge(o_hi, unit_no(g, hh, w) + 1)
                t = slice(c * CH, (c + 1) * CH)
                dve.tensor_tensor(OT[1][:, kind, t], o_raw[:, w % 2, :], f32(OT[0][:, kind, t]), ALU.subtract)\
                    .then_inc(o_lo[0], 1)

            def group_of_heads(g, last):
                for hh, w, more in windows(g, last):
                    nw, nhh = (w + 1) % NW, hh + (w == NW - 1)
                    c = WINDOWS[w][1]
                    for s in range(BLOCKS[w]):
                        if s == 0:
                            dve.wait_ge(exped, tiles_made(g, hh, w))
                            dve.reciprocal(rinv[:, c, :], rsum[:, c, :]).then_inc(inverted, 1)
                        if more or w < NW - 1:
                            for t in range(TPC):
                                if TILE_SLOTS[w][t] == s:
                                    if t == 0:
                                        dve.wait_ge(transposed, block_no(g, hh, w, 0) + unit_no(g, hh, w) + C_T)
                                    row_max(tiles_made(g, hh, w) + t, t % 2, WINDOWS[nw][1], t)
                        here = pieces_of(w, hh, more)
                        if s in here and here[s][0] not in ("LK", "K"):
                            piece(g, hh, w, s, *here[s], piece_bank(hh, w, s, more))
                        if s + 2 < BLOCKS[w]:
                            block_lo(g, hh, w, s + 2)
                        if here.get(s - 1, ("", 0))[0] in ("LK", "K"):
                            piece(g, hh, w, s - 1, *here[s - 1], piece_bank(hh, w, s - 1, more))
                    scale_out(g, hh, w)
                    for j in range(2):
                        if nhh < GROUP:
                            block_lo(g, nhh, nw, j)
                        elif more:
                            block_lo(g + 1, 0, 0, j)
                    if c == 0:
                        out_low(g, hh, w)

            dve.sem_inc(o_scaled, C_OS)
            dve.sem_inc(o_lo[0], C_OL)
            dve.wait_ge(consts_loaded, 64)
            dve.tensor_copy(mask[:, :], vT[:, :]).then_inc(mask_made, 1)
            dve.wait_ge(x_loaded, 16)
            statistics(0)
            normalise(0)
            for n in range(2):
                dve.wait_ge(v_hi, n + 1)
                dve.tensor_tensor(lqT[1][:, n * CH:(n + 1) * CH], bankX[:, :], f32(lqT[0][:, n * CH:(n + 1) * CH]),
                                  ALU.subtract).then_inc(x_free, 1)
            for p in range(ROPES_BEFORE):
                rotate(p, p % RING, p % 2)
            dve.wait_ge(mask_made, 1)
            for n in range(2):
                value_copy(7 + n, n)
            for n in range(2):
                value_lo(3 + n, V, n)
            dve.wait_ge(mask_made, 1)
            for t in range(TPC):
                row_max(t, t % 2, 0, t)
            block_lo(0, 0, 0, 0)
            block_lo(0, 0, 0, 1)

            with dve.Fori(0, KVH - 1) as g:
                group_of_heads(g, False)
            group_of_heads(KVH - 1, True)

            for n in range(TPC):
                add_out(n_piece(KVH - 1, GROUP - 1, 3, 7) + n + 1, n_free(KVH - 1, GROUP - 1, 3, 7) + n + 1, TPC + n)
            for n in range(ND + 2):
                dve.wait_ge(f_hi, n + 1)
                src = bankT[n % 2][:, :]
                if n < ND:
                    hi, lo = f32(WT[0][:, n, :]), WT[1][:, n, :]
                elif n == ND:
                    hi, lo = f32(AT[0]), AT[1]
                    src = src.rearrange("p (k n) -> p k n", k=ND)
                else:
                    hi, lo = f32(BT[0]), BT[1]
                dve.tensor_tensor(lo, src, hi, ALU.subtract).then_inc(f_lo, 1)
            dve.wait_ge(f_ready, ND + 3)
            dve.tensor_copy(rwT, bankT[0][:, 0:ND * E].rearrange("p (k e) -> p k e", k=ND)).then_inc(f_lo, 1)
            statistics(2)
            normalise(NT)
            dve.wait_ge(xt_lo, 2 * NT)
            link(dve.tensor_reduce(xsum, f32(xnT[0][:, :, Q_START:Q_STOP]), AX.X, ALU.add))
            link(dve.tensor_reduce(rot_half[:, 0, ND:2 * ND], f32(xnT[1][:, :, Q_START:Q_STOP]), AX.X, ALU.add))
            link(dve.tensor_tensor(rot_half[:, 0, 2 * ND:3 * ND], xsum, rot_half[:, 0, ND:2 * ND], ALU.add))
            dve.tensor_scalar(xsum, rot_half[:, 0, 2 * ND:3 * ND], 1.0 / (Q_STOP - Q_START), None, ALU.mult)\
                .then_inc(f_lo, 1)
            for i in range(NT):
                dve.tensor_tensor(acc[:, i, :], acc[:, i, :], bias, ALU.add).then_inc(dve_chain, 1)
            chain[0] += NT
            dve.wait_ge(f_ready, ND + 6)
            link(dve.tensor_tensor(soft[:, 0, :], bankO[:, 0:E], r_bias, ALU.add))
            link(dve.tensor_reduce(soft[:, 1, 2:3], soft[:, 0, :], AX.X, ALU.max))
            dve.tensor_scalar(soft[:, 1, 0:1], soft[:, 1, 2:3], -1.0, None, ALU.mult).then_inc(f_free, 1)
            dve.wait_ge(act_step, 3)
            link(dve.reciprocal(soft[:, 1, 3:4], soft[:, 1, 1:2]))
            link(dve.tensor_tensor(soft[:, 3, :], soft[:, 2, :], pick, ALU.mult))
            link(dve.tensor_reduce(soft[:, 4, 0:1], soft[:, 3, :], AX.X, ALU.add))
            link(dve.tensor_scalar(soft[:, 4, 1:2], soft[:, 4, 0:1], soft[:, 1, 3:4], LORA_SCALING, ALU.mult, ALU.mult))
            for n in range(2):
                dve.tensor_scalar(o_raw[:, n, :], scores[0][:, n, :], soft[:, 4, 1:2], None, ALU.mult)\
                    .then_inc(f_free, 1)
            for n in range(2):
                dve.wait_ge(f_hi, ND + 3 + n)
                t = slice(n * CH, (n + 1) * CH)
                dve.tensor_tensor(tT[1][:, t], o_raw[:, n, :], f32(tT[0][:, t]), ALU.subtract).then_inc(f_lo, 1)
            for i in range(NT):
                dve.wait_ge(f_ready, ND + 6 + i + 1)
                dve.wait_ge(dve_chain, chain[0])
                dve.tensor_tensor(acc[:, i, :], scores[1][:, i % 2, :], acc[:, i, :], ALU.add).then_inc(y_done, 1)

        @block.gpsimd
        def _(pool):
            def subtract(place, src, hi):
                return pool.tensor_tensor(place, src, f32(hi), ALU.subtract)

            def rope_add(no, slot, n):
                pool.wait_ge(rope_half, no + 1)
                pool.tensor_tensor(rot[:, slot, :], rot[:, slot, :], cos[:, chunk(n)], ALU.mult).then_inc(rope_cos, 1)
                pool.wait_ge(rope_cos, no + 1)
                pool.tensor_tensor(rot[:, slot, :], rot[:, slot, :], rot_half[:, n, :], ALU.add).then_inc(rope_sum, 1)

            def rope_low(no, slot, places, at):
                pool.wait_ge(rope_hi, no + 1)
                subtract(places[1][at], rot[:, slot, :], places[0][at]).then_inc(rope_lo, 1)

            def weights_low(no, slot, places):
                pool.wait_ge(w_hi, no + 1)
                src = stage[:, slot, 0:HD if places is Wlk else CH]
                if len(places[0].shape) == 3:
                    subtract(places[1][:, :, :], src.rearrange("p (k n) -> p k n", k=ND), places[0][:, :, :])\
                        .then_inc(w_lo, 1)
                else:
                    subtract(places[1][:, :], src, places[0][:, :]).then_inc(w_lo, 1)

            def ropes(g, hh, name, places, at):
                for n in range(2):
                    rope_add(rope_no(g, hh, name, n), rope_no(0, hh, name, n) % RING, n)
                for n in range(2):
                    rope_low(rope_no(g, hh, name, n), rope_no(0, hh, name, n) % RING, places, at(n))

            ALL = slice(None)

            def chunk(n):
                return slice(n * CH, (n + 1) * CH)

            def out_low(g, hh, w):
                kind, c = WINDOWS[w]
                pool.wait_ge(o_hi, unit_no(g, hh, w) + 1)
                at = (ALL, kind, chunk(c))
                subtract(OT[1][at], o_raw[:, w % 2, :], OT[0][at]).then_inc(o_lo[1], 1)

            def group_of_heads(g, last):
                for hh, w, more in windows(g, last):
                    if w == 0:
                        ropes(g, hh, "LK", LKT, lambda n: (ALL, chunk(n)))
                        if more and hh == GROUP - 1:
                            for name, places in (("Wk", Wk), ("Wv", Wv)):
                                weights_low(load_no(g, hh, name), load_no(0, hh, name) % 2, places)
                    if w == 1 and more:
                        weights_low(load_no(g, hh, "Wq"), load_no(0, hh, "Wq") % 2, Wq)
                    if w == 1:
                        out_low(g, hh, w)
                    if w == 2:
                        no, at = ((load_no(g, hh, "Wo"), load_no(0, hh, "Wo")) if more else
                                  (load_no(g, hh, "Wk"), load_no(0, hh, "Wk")))
                        for k, places in enumerate((Wo, Wlo)):
                            weights_low(no + k, (at + k) % 2, places)
                    q_at = lambda n: (ALL, (hh + 1) % 2, chunk(n))
                    if w == 2 and more:
                        k_no = [(rope_no(g, hh, "K", n), rope_no(0, hh, "K", n) % RING) for n in range(2)]
                        if hh == GROUP - 1:
                            rope_add(*k_no[0], 0)
                            rope_add(*k_no[1], 1)
                            rope_low(*k_no[0], KT, (ALL, chunk(0)))
                        rope_add(rope_no(g, hh, "Q", 0), rope_no(0, hh, "Q", 0) % RING, 0)
                        if hh == GROUP - 1:
                            rope_low(*k_no[1], KT, (ALL, chunk(1)))
                    if w == 3 and more:
                        rope_low(rope_no(g, hh, "Q", 0), rope_no(0, hh, "Q", 0) % RING, QT, q_at(0))
                        rope_add(rope_no(g, hh, "Q", 1), rope_no(0, hh, "Q", 1) % RING, 1)
                        rope_low(rope_no(g, hh, "Q", 1), rope_no(0, hh, "Q", 1) % RING, QT, q_at(1))
                        for name, places in (("Wlk", Wlk), ("Wlv", Wlv)):
                            weights_low(load_no(g, hh, name), load_no(0, hh, name) % 2, places)
                    if w == 3:
                        out_low(g, hh, w)

            pool.sem_inc(o_lo[1], C_OL)
            for tensor in (*PTD, *OT, *Wo, *Wlo):
                flat = tensor[tuple([ALL] * len(tensor.shape))]
                ins = pool.memset(f32(flat), 0.0)
            ins.then_inc(cleared, 1)
            for no, places in enumerate((Wlv, Wq, Wk, Wv)):
                weights_low(no, no % 2, places)
            weights_low(4, 0, Wlk)
            weights_low(5, 1, Wlv)
            for p in range(ROPES_BEFORE):
                n = p % 2
                rope_add(p, p % RING, n)
                rope_low(p, p % RING, (QT, KT)[p // 2], ((ALL, 0, chunk(n)), (ALL, chunk(n)))[p // 2])

            with pool.Fori(0, KVH - 1) as g:
                group_of_heads(g, False)
            group_of_heads(KVH - 1, True)


_INS = ["L0_attn_hidden_states", "L0_attn_w_q", "L0_attn_w_k", "L0_attn_w_v", "L0_attn_w_o", "L0_attn_w_lq",
        "L0_attn_w_lk", "L0_attn_w_lv", "L0_attn_w_lo", "L0_ffn_W", "L0_ffn_b", "L0_ffn_A", "L0_ffn_B",
        "L0_ffn_router_W", "L0_ffn_router_b"]


def shape_constants():
    inv_freq = (1.0 / THETA ** (np.arange(0, HD, 2, dtype=np.float32) / HD)).astype(np.float32)
    freqs = np.outer(np.arange(S, dtype=np.float32), inv_freq).astype(np.float32)
    cos = np.tile(np.cos(freqs).T, (2, 1)).astype(np.float32)
    sin = np.concatenate([np.sin(freqs).T, -np.sin(freqs).T], 0).astype(np.float32)
    mask = np.zeros((P, S), np.float32)
    mask[:, S - P:] = np.where(np.tril(np.ones((P, P), bool)), 0.0, MASKED)
    pick = (np.arange(P)[:, None] // R == np.arange(E)[None, :]).astype(np.float32)
    return {"cos": cos, "sin": sin, "mask": mask, "ident": np.eye(P, dtype=np.float32), "pick": pick}


def kernel(**inputs):
    import concourse.bacc as bacc
    from concourse.bass_utils import run_bass_kernel_spmd

    nc = bacc.Bacc("TRN2", target_bir_lowering=False, num_devices=1)
    arrays, args = {}, []
    for name in _INS:
        arrays[f"in_{name}"] = np.ascontiguousarray(inputs[name])
    for name, a in shape_constants().items():
        arrays[f"const_{name}"] = np.ascontiguousarray(a)
    for name, a in arrays.items():
        args.append(nc.dram_tensor(name, a.shape, mybir.dt.from_np(a.dtype), kind="ExternalInput").ap())
    args.append(nc.dram_tensor("out", (1, S, D), F32, kind="ExternalOutput").ap())
    attn_ffn_kernel(nc, *args)
    result = run_bass_kernel_spmd(nc, [arrays], core_ids=[0])
    return result.results[0]["out"]
```

```python
from contextlib import ExitStack

import numpy as np

import concourse.bass as bass
from concourse import mybir

F32 = mybir.dt.float32
F32R = mybir.dt.float32r
ALU = mybir.AluOpType
ACT = mybir.ActivationFunctionType
AX = mybir.AxisListType

P = 128
S, D = 1024, 512
H, KVH, HD = 32, 8, 128
E, R, O = 8, 16, 512
GROUP = H // KVH
NT, ND = S // P, D // P
CH = 512
TPC = CH // P
HALF = HD // 2
THETA = 10000.0
SCALE = 1.0 / float(np.sqrt(HD))
EPS = 1e-5
LORA_SCALING = 32 / 16
Q_START, Q_STOP = 34 + 72 + 1, S - 1
MASKED = -3.0e38
RING = 3

WINDOWS = [(0, 0), (0, 1), (1, 0), (1, 1)]
NW = len(WINDOWS)
BLOCKS = [TPC * (c + 1) for _, c in WINDOWS]
BLOCK0 = [sum(BLOCKS[:w]) for w in range(NW)]
BPH = sum(BLOCKS)
TILE_SLOTS = [[0, 1, 1, 2], [1, 2, 4, 6], [0, 0, 1, 1], [3, 4, 5, 6]]


def pieces_of(w, hh, more):
    next_group = more and hh == GROUP - 1
    if w == 0:
        return {0: ("LK", 0), 1: ("LK", 1), 3: ("LV", 0)}
    if w == 1:
        return {0: ("LV", 1), 1: ("OUT1", 0), 2: ("OUT1", 1), 3: ("LVT", 0), 5: ("LVT", 1), 6: ("OUT1", 2),
                7: ("OUT1", 3)}
    if w == 2:
        ahead = {0: ("K", 0), 1: ("K", 1), 2: ("V", 0)} if next_group else {}
        return {**ahead, 3: ("Q", 0)} if more else {}
    ahead = {0: ("Q", 1)} if more else {}
    if next_group:
        ahead.update({1: ("V", 1), 2: ("VT", 0), 3: ("VT", 1)})
    slots = (4, 5, 6, 7) if hh == GROUP - 1 else (2, 4, 5, 7)
    return {**ahead, **{s: ("OUT0", n) for n, s in enumerate(slots)}}


ROPE = ("Q", "K", "LK")


def number_pieces():
    at, dve_at, n, m = {}, {}, 0, 0
    for hh in range(GROUP):
        for w in range(NW):
            for s, (name, _) in sorted(pieces_of(w, hh, True).items()):
                at[hh, w, s] = n
                n += 1
                if name not in ROPE:
                    dve_at[hh, w, s] = m
                    m += 1
    return at, n, dve_at, m


X_AT, XPG, FREE_AT, FREES_PER_GROUP = number_pieces()
X_BEFORE = 10
FREES_BEFORE = 6
ROPES_BEFORE = 4
ROPES_PER_GROUP = 2 * (2 * GROUP + 1)
VTS_PER_GROUP = 2 * (GROUP + 1)
LOADS_BEFORE = 6
LOADS_PER_GROUP = 5 * GROUP + 2

C_T, C_PV, C_OS, C_OL = 1, 3, 2, 1


def p_offset(c, t):
    return P * sum(TPC * c + k + 1 for k in range(t))


def block_columns(c, j):
    return P * max(0, j - TPC * c)


def attn_ffn_kernel(nc, x_in, w_q, w_k, w_v, w_o, w_lq, w_lk, w_lv, w_out_latent, W, b, A, B, router_W, router_b,
                    cos_in, sin_in, mask_in, ident_in, pick_in,
                    averaged_in, out, inverses):
    with ExitStack() as ctx:
        def sb(name, shape, dt=F32):
            return ctx.enter_context(nc.sbuf_tensor(name, shape, dt))

        def pair(name, shape):
            return sb(name + "_hi", shape, F32R), sb(name + "_lo", shape, F32R)

        def sem(name):
            return ctx.enter_context(nc.semaphore(name))

        cos = sb("cos", [P, S])
        sin = sb("sin", [P, S])
        mask = sb("mask", [P, S], mybir.dt.bfloat16)
        ident = sb("ident", [P, P])
        acc = sb("acc", [P, NT, D])
        xnT = pair("xnT", [P, ND, S])
        lqT = pair("lqT", [P, S])
        QT = pair("QT", [P, 2, S])
        KT = pair("KT", [P, S])
        LKT = pair("LKT", [P, S])
        V = pair("V", [P, NT, HD])
        LV = pair("LV", [P, NT, HD])
        vT = sb("vT", [P, S])
        probs = [sb(f"probs{c}", [P, p_offset(c, TPC)]) for c in range(2)]
        PT = pair("PT", [P, 2, CH])
        PTD = pair("PTD", [P, 2 * P])
        OT = pair("OT", [P, 2, S])
        o_raw = sb("o_raw", [P, 2, CH])
        inv_b = sb("inv_b", [P, 2, CH])
        rot_half = sb("rot_half", [P, 2, CH])
        rot = sb("rot", [P, RING, CH])
        Wq = pair("Wq", [P, ND, HD])
        Wk = pair("Wk", [P, ND, HD])
        Wv = pair("Wv", [P, ND, HD])
        Wlv = pair("Wlv", [P, ND, HD])
        Wlk = pair("Wlk", [P, HD])
        Wo = pair("Wo", [P, D])
        Wlo = pair("Wlo", [P, D])
        stage = sb("stage", [P, 2, CH])
        nmax = sb("nmax", [P, 2, TPC])
        rsum = sb("rsum", [P, 2, TPC])
        rinv = sb("rinv", [P, 2, TPC])
        stats = inv_b[:, 0, 64:64 + 6 * NT].rearrange("p (i n) -> p i n", n=6)
        mv = inv_b[:, 0, 128:128 + 2 * NT].rearrange("p (i n) -> p i n", n=2)
        std = inv_b[:, 0, 192:192 + 4 * NT].rearrange("p (n i) -> p n i", i=NT)

        scores = [ctx.enter_context(nc.psum_tensor(f"scores{i}", [P, 2, CH], F32)) for i in range(2)]
        bankT = [ctx.enter_context(nc.psum_tensor(f"bankT{i}", [P, CH], F32)) for i in range(2)]
        bankO = ctx.enter_context(nc.psum_tensor("bankO", [P, CH], F32))
        bankX = ctx.enter_context(nc.psum_tensor("bankX", [P, CH], F32))
        banksX = [bankX[:, :], scores[1][:, 1, :]]

        x_loaded, w_loaded = [sem("x_loaded0"), sem("x_loaded1")], [sem("w_loaded0"), sem("w_loaded1")]
        consts_loaded = sem("consts_loaded")
        ident_loaded, ffn_loaded, router_loaded = sem("ident_loaded"), sem("ffn_loaded"), sem("router_loaded")
        out_stored = sem("out_stored")
        scored, transposed, pv_done, x_ready = sem("scored"), sem("transposed"), sem("pv_done"), sem("x_ready")
        row_maxed, pt_lo, x_free, o_scaled, inverted = (sem("row_maxed"), sem("pt_lo"), sem("x_free"),
                                                        sem("o_scaled"), sem("inverted"))
        dve_step, act_step = sem("dve_step"), sem("act_step")
        exped, pt_hi, w_hi, rope_hi, o_hi, v_hi = (sem("exped"), sem("pt_hi"), sem("w_hi"), sem("rope_hi"),
                                                   sem("o_hi"), sem("v_hi"))
        inverses_stored, inverses_loaded = sem("inverses_stored"), sem("inverses_loaded")
        rope_raw, rope_half, rope_cos = sem("rope_raw"), sem("rope_half"), sem("rope_cos")
        rope_sum, rope_lo, o_lo, w_lo, cleared = (sem("rope_sum"), sem("rope_lo"), [sem("o_lo0"), sem("o_lo1")], sem("w_lo"),
                                                  sem("cleared"))
        xn_made, xt_ready, xt_hi, xt_lo = sem("xn_made"), sem("xt_ready"), sem("xt_hi"), sem("xt_lo")
        f_ready, f_hi, f_lo, f_free = sem("f_ready"), sem("f_hi"), sem("f_lo"), sem("f_free")
        f_chain, mask_made, score_seen = sem("f_chain"), sem("mask_made"), sem("score_seen")
        xt_used, y_ready, y_added, y_biased = sem("xt_used"), sem("y_ready"), sem("y_added"), sem("y_biased")

        f32 = lambda ap: ap.bitcast(F32)

        def block_no(g, hh, w, j):
            return (g * GROUP + hh) * BPH + BLOCK0[w] + j

        def unit_no(g, hh, w):
            return (g * GROUP + hh) * NW + w

        def n_out_low(g, hh, kind):
            return (g * GROUP + hh) * 2 + kind + 1 + C_OL

        def n_transposed(g, hh, w, j):
            return block_no(g, hh, w, j) + 1 + C_T

        def n_piece(g, hh, w, s):
            skipped = 8 if isinstance(g, int) and g == KVH - 1 and (hh, w) == (GROUP - 1, NW - 1) else 0
            return g * XPG + (X_BEFORE + X_AT[hh, w, s] + 1 - skipped)

        def n_free(g, hh, w, s):
            skipped = 4 if isinstance(g, int) and g == KVH - 1 and (hh, w) == (GROUP - 1, NW - 1) else 0
            return g * FREES_PER_GROUP + (FREES_BEFORE + FREE_AT[hh, w, s] + 1 - skipped)

        def piece_bank(hh, w, s, more):
            return sorted(pieces_of(w, hh, more)).index(s) % 2 if w in (1, 3) else 0

        def bank_x_taken(eng, g, hh, w, s, last):
            bank = piece_bank(hh, w, s, not (last and hh == GROUP - 1))
            ahead = [(h2, w2, s2, name) for h2, w2, more in windows(g, last) for s2, name in
                     sorted(pieces_of(w2, h2, more).items())
                     if (h2, w2, s2) < (hh, w, s) and piece_bank(h2, w2, s2, more) == bank]
            if bank and not (ahead and ahead[-1][:2] == (hh, w)):
                eng.wait_ge(row_maxed, tiles_made(g, hh, w))
                return
            if not ahead:
                eng.wait_ge(x_free, g * FREES_PER_GROUP + FREES_BEFORE)
                return
            h2, w2, s2, (name, n) = ahead[-1]
            if name in ROPE:
                eng.wait_ge(rope_raw, rope_no(g, h2, name, n) + 1)
            else:
                eng.wait_ge(x_free, n_free(g, h2, w2, s2))

        def rope_no(g, hh, name, n):
            base = g * ROPES_PER_GROUP + (ROPES_BEFORE + 4 * hh)
            return base + {"LK": 0, "K": 2, "Q": 4 if hh == GROUP - 1 else 2}[name] + n

        def vt_no(g, hh, name, n):
            return g * VTS_PER_GROUP + (2 + 2 * hh + {"LVT": 0, "VT": 2}[name] + n)

        def load_no(g, hh, name):
            order = (["Wk", "Wv"] if hh == GROUP - 1 else []) + ["Wq", "Wo", "Wlo", "Wlk", "Wlv"]
            return g * LOADS_PER_GROUP + (LOADS_BEFORE + 5 * hh + order.index(name))

        def n_latent_load(g, hh, name):
            before = g * LOADS_PER_GROUP + (LOADS_BEFORE + 5 * hh)
            return before - (1 if name == "Wlk" else 0)

        def tiles_made(g, hh, w):
            return TPC * (unit_no(g, hh, w) + 1)

        def last_block(g, hh, w):
            return block_no(g, hh, w, BLOCKS[w] - 1)

        def windows(g, last):
            for hh in range(GROUP):
                for w in range(NW):
                    yield hh, w, not (last and hh == GROUP - 1)

        def ring_slot(hh, w, j):
            ahead = sum(BLOCKS[k] - 1 for k in range(w)) + j
            return None if j == BLOCKS[w] - 1 else ahead % 2

        def pt_place(half, hh, w, j):
            slot = ring_slot(hh, w, j)
            if slot is None:
                return PTD[half][:, P:2 * P]
            return PT[half][:, slot, block_columns(WINDOWS[w][1], j):CH]

        def tile_view(ap, c):
            return ap if c == 0 else ap.rearrange("p (a n) -> p a n", a=2)

        def tile_bank(n, c, width):
            return scores[n % 2][:, 0, 0:width] if c == 0 else scores[n % 2][:, :, 0:width // 2]

        def prob_tile(c, t):
            width = P * (TPC * c + t + 1)
            return probs[c][:, p_offset(c, t):p_offset(c, t) + width]

        n_ffn_loads = 4 + ND
        W_raw = [(cos, sin)[k // 2][:, k % 2 * D:(k % 2 + 1) * D] for k in range(ND)]
        A_raw = vT[:, 0:D]
        B_raw = vT[:, D:2 * D].rearrange("p (k c) -> p k c", k=ND)
        rw_raw = rot[0:E, 0, :]
        WT = [h[:, :, :].rearrange("p a b -> p (a b)").rearrange("p (k n) -> p k n", k=ND) for h in QT]
        AT = [h[:, 0:CH].rearrange("p (k n) -> p k n", k=ND) for h in LKT]
        BT = [h[:, 0:O] for h in KT]
        rwT = inv_b[:, 0, 0:ND * E].rearrange("p (k e) -> p k e", k=ND)
        bias = probs[0][:, D:2 * D]
        r_bias = probs[0][:, 2 * D:2 * D + E]
        pick = probs[0][:, 2 * D + E:2 * D + 2 * E]
        averaged = probs[0][:, 2 * D + 2 * E:2 * D + 2 * E + NT]
        tT = lqT
        xsum = rot_half[:, 0, 0:ND]
        soft = rot_half[:, 0, 64:64 + 8 * E].rearrange("p (k e) -> p k e", e=E)
        four = [scores[k // 2][:, k % 2, :] for k in range(4)]
        N_JOBS = ND + 3

        block = ctx.enter_context(nc.Block())

        @block.sync
        def _(sp):
            def load_x(half):
                tiles = slice(half * TPC, (half + 1) * TPC)
                sp.dma_start(acc[:, tiles, :], x_in[0, half * CH:(half + 1) * CH, :].rearrange("(i p) d -> p i d", p=P))\
                    .then_inc(x_loaded[half], 16)

            def load(no, slot, src):
                if not (isinstance(no, int) and no < 2):
                    sp.wait_ge(w_lo, no - 1)
                width = CH if len(src.shape) == 3 or src.shape[1] == CH else HD
                place = stage[:, slot, 0:width]
                if len(src.shape) == 3:
                    place = place.rearrange("p (k n) -> p k n", k=ND)
                sp.dma_start(place, src).then_inc(w_loaded[slot], 16)

            def columns(w, at):
                return w[:, bass.ds(at, HD)].rearrange("(k p) n -> p k n", p=P)

            load_x(0)
            sp.dma_start(ident[:, :], ident_in).then_inc(ident_loaded, 16)
            load(0, 0, columns(w_q, 0))
            load(1, 1, columns(w_k, 0))
            load_x(1)
            for place, src in ((cos, cos_in), (sin, sin_in), (vT, mask_in)):
                sp.dma_start(place[:, :], src).then_inc(consts_loaded, 16)
            for no, src in enumerate((columns(w_lq, 0), columns(w_v, 0), w_lk[:, 0:HD], columns(w_lv, 0))):
                load(no + 2, no % 2, src)

            def spread_inverses(g, hh, w):
                unit, c = unit_no(g, hh, w), WINDOWS[w][1]
                sp.wait_ge(inverted, unit + 1)
                sp.dma_start(inverses[w % 2].rearrange("(p t) -> p t", p=P), rinv[:, c, :]).then_inc(inverses_stored, 16)
                sp.wait_ge(inverses_stored, 16 * (unit + 1))
                sp.wait_ge(o_scaled, unit - 1 + C_OS)
                sp.dma_start(inv_b[:, w % 2, :], inverses[w % 2].rearrange("(a n) -> a n", a=1).broadcast_to([P, CH]))\
                    .then_inc(inverses_loaded, 16)

            def group_of_heads(g, last):
                for hh in range(GROUP):
                    more = not (last and hh == GROUP - 1)
                    here = (g * GROUP + hh) * HD
                    after = (g * GROUP + hh + 1) * HD

                    def fetch(name, src):
                        no = load_no(g, hh, name)
                        load(no, load_no(0, hh, name) % 2, src)

                    spread_inverses(g, hh, 0)
                    if more:
                        if hh == GROUP - 1:
                            fetch("Wk", columns(w_k, (g + 1) * HD))
                            fetch("Wv", columns(w_v, (g + 1) * HD))
                        fetch("Wq", columns(w_q, after))
                        if hh < GROUP - 1:
                            fetch("Wo", w_o[bass.ds(here, HD), :])
                    if not more:
                        for k, src in enumerate((w_o[bass.ds(here, HD), :], w_out_latent[bass.ds(here, HD), :])):
                            load(load_no(g, hh, "Wk") + k, (load_no(0, hh, "Wk") + k) % 2, src)
                        spread_inverses(g, hh, 1)
                        sp.wait_ge(rope_lo, rope_no(g, hh, "LK", 1) + 1)
                        for k, table in enumerate((cos, sin)):
                            sp.dma_start(table[:, :].rearrange("p (k n) -> p k n", k=2),
                                         W[2 * k * P:2 * (k + 1) * P, :].rearrange("(k p) n -> p k n", p=P))\
                                .then_inc(ffn_loaded, 16)
                        sp.dma_start(rw_raw, router_W).then_inc(ffn_loaded, 16)
                        sp.wait_ge(x_ready, n_piece(g, hh, 1, 5))
                        sp.dma_start(A_raw, A.rearrange("e r d -> (e r) d")).then_inc(ffn_loaded, 16)
                        for k in range(ND):
                            sp.dma_start(B_raw[:, k, :].rearrange("p (e r) -> p e r", e=E),
                                         B[:, k * P:(k + 1) * P, :].rearrange("e p r -> p e r")).then_inc(ffn_loaded, 16)
                        spread_inverses(g, hh, 2)
                        sp.wait_ge(transposed, n_transposed(g, hh, 2, BLOCKS[2] - 1))
                        sp.dma_start(bias, b.rearrange("(a n) -> a n", a=1).broadcast_to([P, D]))\
                            .then_inc(router_loaded, 16)
                        sp.dma_start(r_bias, router_b.rearrange("(a n) -> a n", a=1).broadcast_to([P, E]))\
                            .then_inc(router_loaded, 16)
                        sp.dma_start(pick, pick_in).then_inc(router_loaded, 16)
                        sp.dma_start(averaged, averaged_in).then_inc(router_loaded, 16)
                        spread_inverses(g, hh, 3)
                        continue
                    spread_inverses(g, hh, 1)
                    if hh == GROUP - 1:
                        fetch("Wo", w_o[bass.ds(here, HD), :])
                    fetch("Wlo", w_out_latent[bass.ds(here, HD), :])
                    spread_inverses(g, hh, 2)
                    fetch("Wlk", w_lk[:, bass.ds(after, HD)])
                    fetch("Wlv", columns(w_lv, after))
                    spread_inverses(g, hh, 3)

            with sp.Fori(0, KVH - 1) as g:
                group_of_heads(g, False)
            group_of_heads(KVH - 1, True)

            for i in range(NT):
                sp.wait_ge(y_added, NT + i + 1)
                sp.dma_start(out[0, i * P:(i + 1) * P, :], acc[:, i, :]).then_inc(out_stored, 16)
            sp.wait_ge(out_stored, 16 * NT)

        @block.tensor
        def _(pe):
            def mm3(place, left, right, start, stop):
                pe.matmul(place, left[1], right[0], start=start, stop=False)
                pe.matmul(place, left[0], right[1], start=False, stop=False)
                return pe.matmul(place, left[0], right[0], start=False, stop=stop)

            def both(pair_, *index):
                return [h[index] for h in pair_]

            ALL = slice(None)

            def normalised_transpose(made, i):
                pe.wait_ge(xn_made, made + i + 1)
                if i >= 2:
                    pe.wait_ge(xt_lo, made + i - 1)
                for k in range(ND):
                    mm = pe.transpose(bankT[i % 2][:, k * P:(k + 1) * P],
                                      o_raw[:, i % 2, k * P:(k + 1) * P], ident[:, :])
                mm.then_inc(xt_ready, 1)

            def project(weights, n, bank=0, place=None):
                for k in range(ND):
                    mm = mm3(banksX[bank] if place is None else place, both(weights, ALL, k, ALL), both(xnT, ALL, k, slice(n * CH, n * CH + CH)),
                             k == 0, k == ND - 1)
                return mm

            def value_transposes(n, bank=0):
                for i in range(TPC):
                    mm = pe.transpose(banksX[bank][:, i * P:(i + 1) * P],
                                      vT[:, (n * TPC + i) * P:(n * TPC + i + 1) * P], ident[:, :])
                return mm

            def out_tile(c, i, bank=0):
                rows = slice((TPC * c + i) * P, (TPC * c + i + 1) * P)
                mm3(banksX[bank], both(OT, ALL, 0, rows), both(Wo, ALL, ALL), True, False)
                return mm3(banksX[bank], both(OT, ALL, 1, rows), both(Wlo, ALL, ALL), False, True)

            def score_tile(no, parity, head, kind, c, t):
                if not (isinstance(no, int) and no < 2):
                    pe.wait_ge(row_maxed, no - 1)
                i = TPC * c + t
                width = (i + 1) * P
                keys = LKT if kind else KT
                query = both(QT, ALL, head % 2, slice(i * P, (i + 1) * P))
                if c == 0:
                    n = max(width, 2 * P)
                    mm = mm3(scores[parity][:, 0, 0:n], query, both(keys, ALL, slice(0, n)), True, True)
                else:
                    for a in range(2):
                        part = slice(a * width // 2, (a + 1) * width // 2)
                        mm = mm3(scores[parity][:, a, 0:width // 2], query, both(keys, ALL, part), True, True)
                mm.then_inc(scored, 1)

            def transpose_block(g, hh, w, j):
                c = WINDOWS[w][1]
                no = block_no(g, hh, w, j)
                if j == 0:
                    pe.wait_ge(exped, tiles_made(g, hh, w))
                if not (isinstance(no, int) and no < 2):
                    pe.wait_ge(pt_lo, no - 1)
                for t in range(max(0, j - TPC * c), TPC):
                    at = p_offset(c, t) + j * P
                    mm = pe.transpose(bankT[j % 2][:, t * P:(t + 1) * P],
                                      probs[c][:, at:at + P], ident[:, :])
                mm.then_inc(transposed, 1)

            def pv_block(g, hh, w, j):
                kind, c = WINDOWS[w]
                no = block_no(g, hh, w, j)
                pe.wait_ge(pt_lo, no + 1)
                if j == 0:
                    pe.wait_ge(o_scaled, unit_no(g, hh, w) + C_OS)
                values = both(LV if kind else V, ALL, j, ALL)
                if j == BLOCKS[w] - 1:
                    mm = mm3(bankO[:, CH - 2 * P:CH], values, both(PTD, ALL, ALL), False, True)
                else:
                    at = block_columns(c, j)
                    mm = mm3(bankO[:, at:CH], values, both(PT, ALL, ring_slot(hh, w, j), slice(at, CH)), j == 0, False)
                mm.then_inc(pv_done, 1)

            def piece(g, hh, w, s, name, n):
                bank_x_taken(pe, g, hh, w, s, g_last[0])
                bank = piece_bank(hh, w, s, not (g_last[0] and hh == GROUP - 1))
                if name == "LK":
                    pe.wait_ge(w_lo, n_latent_load(g, hh, "Wlk"))
                    mm = mm3(bankX[:, :], both(Wlk, ALL, ALL), both(lqT, ALL, slice(n * CH, n * CH + CH)), True, True)
                elif name == "LV":
                    pe.wait_ge(w_lo, n_latent_load(g, hh, "Wlv"))
                    mm = project(Wlv, n, bank)
                elif name in ("LVT", "VT"):
                    mm = value_transposes(n, bank)
                elif name == "Q":
                    pe.wait_ge(w_lo, load_no(g, hh, "Wq") + 1)
                    mm = project(Wq, n, bank)
                elif name == "K":
                    pe.wait_ge(w_lo, load_no(g, hh, "Wk") + 1)
                    mm = project(Wk, n, bank)
                elif name == "V":
                    pe.wait_ge(w_lo, load_no(g, hh, "Wv") + 1)
                    mm = project(Wv, n, bank)
                elif name == "OUT0":
                    pe.wait_ge(w_lo, out_weights(g, hh, g_last[0]))
                    pe.wait_ge(o_lo[0], n_out_low(g, hh, 1))
                    mm = out_tile(0, n, bank)
                else:
                    pe.wait_ge(o_lo[1], n_out_low(g, hh, 0) - 1)
                    mm = out_tile(1, n, bank)
                mm.then_inc(x_ready, 1)

            def ffn_transpose(n):
                if n == 0:
                    pe.wait_ge(ffn_loaded, 16 * n_ffn_loads)
                    pe.wait_ge(row_maxed, H * NW * TPC)
                if n >= 3:
                    pe.wait_ge(f_lo, n - 2)
                for m in range(ND):
                    if n < ND + 2:
                        src = (W_raw[m][:, n * P:(n + 1) * P] if n < ND else A_raw[:, m * P:(m + 1) * P] if n == ND
                               else B_raw[:, m, :])
                        mm = pe.transpose(four[n % 3][:, m * P:(m + 1) * P], src, ident[:, :])
                    else:
                        mm = pe.transpose(four[n % 3][:, m * E:(m + 1) * E], rw_raw[:, m * P:(m + 1) * P],
                                          ident[0:E, 0:E])
                mm.then_inc(f_ready, 1)

            g_last = [False]

            def out_weights(g, hh, last):
                if last and hh == GROUP - 1:
                    return load_no(g, hh, "Wk") + 2
                return load_no(g, hh, "Wlo") + 1

            def group_of_heads(g, last):
                g_last[0] = last
                for hh, w, more in windows(g, last):
                    nw, nhh = (w + 1) % NW, hh + (w == NW - 1)

                    def next_transposes(j):
                        if nhh < GROUP:
                            transpose_block(g, nhh, nw, j)
                        elif more:
                            transpose_block(g + 1, 0, 0, j)

                    for s in range(BLOCKS[w]):
                        if more or w < NW - 1:
                            for t in range(TPC):
                                if TILE_SLOTS[w][t] != s:
                                    continue
                                no = tiles_made(g, hh, w) + t
                                if t == 0 and w in (1, 2):
                                    pe.wait_ge(rope_lo, rope_no(g, hh, "LK", w - 1) + 1)
                                if t == 0 and w == 3:
                                    pe.wait_ge(rope_lo, rope_no(g, hh, "Q", 0) + 1)
                                if t == 0 and w == 0:
                                    pe.wait_ge(rope_lo, rope_no(g, hh, "LK", 0))
                                if t == 1 and w == 0:
                                    pe.wait_ge(x_free, g * FREES_PER_GROUP + FREES_BEFORE if hh == 0 else
                                               n_free(g, hh - 1, 3, 7))
                                if t == 1 and w == 2:
                                    pe.wait_ge(x_free, n_free(g, hh, 1, 7))
                                score_tile(no, t % 2, nhh, WINDOWS[nw][0], WINDOWS[nw][1], t)
                        if s in pieces_of(w, hh, more):
                            piece(g, hh, w, s, *pieces_of(w, hh, more)[s])
                        if w == NW - 1 and not more and s < N_JOBS:
                            ffn_transpose(s)
                        if s + 2 < BLOCKS[w]:
                            transpose_block(g, hh, w, s + 2)
                        if s == 0 and w in (0, 2):
                            if w == 2:
                                pe.wait_ge(x_free, n_free(g, hh, 1, 5))
                            elif hh == 0:
                                pe.wait_ge(x_free, g * FREES_PER_GROUP + FREES_BEFORE)
                        if s == BLOCKS[w] - 1:
                            next_transposes(0)
                        pv_block(g, hh, w, s)
                    next_transposes(1)

            pe.sem_inc(transposed, C_T)
            pe.sem_inc(pv_done, C_PV)
            pe.wait_ge(ident_loaded, 16)
            for i in range(TPC):
                normalised_transpose(0, i)
            places = (Wq, Wk, Wlv, Wv)
            for n in range(2):
                for x, weights in enumerate(places):
                    if n == 0:
                        pe.wait_ge(w_lo, x + 1)
                        pe.wait_ge(xt_lo, TPC)
                    elif x == 0:
                        pe.wait_ge(xt_lo, NT)
                    if n:
                        pe.wait_ge(*((rope_raw, x + 1) if x < 2 else (x_free, x - 1)))
                    project(weights, n, place=four[x]).then_inc(x_ready, 1)
                    if n == 0 and x < 2:
                        normalised_transpose(0, TPC + 2 * x)
                        normalised_transpose(0, TPC + 2 * x + 1)
            pe.wait_ge(rope_raw, 4)
            pe.wait_ge(rope_lo, 2)
            for t in range(TPC):
                if t == 1:
                    pe.wait_ge(x_free, 3)
                score_tile(t, t % 2, 0, 0, 0, t)
            for n in range(2):
                pe.wait_ge(x_free, 4)
                value_transposes(n, n).then_inc(x_ready, 1)
            transpose_block(0, 0, 0, 0)
            transpose_block(0, 0, 0, 1)

            with pe.Fori(0, KVH - 1) as g:
                group_of_heads(g, False)
            group_of_heads(KVH - 1, True)

            for n in range(TPC):
                pe.wait_ge(x_free, n_free(KVH - 1, GROUP - 1, 3, 7) + n - 1)
                if n == 0:
                    pe.wait_ge(o_lo[1], 2 * H + C_OL)
                out_tile(1, n, n % 2).then_inc(x_ready, 1)

            def tail_tile(i):
                if i == 0:
                    pe.wait_ge(pt_lo, H * BPH)
                    pe.wait_ge(router_loaded, 16 * 4)
                    pe.wait_ge(x_free, n_free(KVH - 1, GROUP - 1, 3, 7) + TPC)
                normalised_transpose(NT, i)
                for k in range(ND):
                    mm = pe.matmul(bankX[:, k:k + 1], o_raw[:, i % 2, k * P:(k + 1) * P], averaged[:, i:i + 1],
                                   start=(i + k == 0), stop=(i + k == NT + ND - 2))
                mm.then_inc(xt_used, 1)

            def y_bank(n):
                if n >= 4:
                    pe.wait_ge(y_added, n - 3)
                return four[n % 4]

            def base_tile(i):
                place = y_bank(i)
                if i == 0:
                    pe.wait_ge(f_lo, N_JOBS)
                pe.wait_ge(xt_lo, NT + i + 1)
                for k in range(ND):
                    mm = mm3(place, both(xnT, ALL, k, slice(i * P, (i + 1) * P)), both(WT, ALL, k, ALL), k == 0, k == ND - 1)
                mm.then_inc(y_ready, 1)

            def inner(n, place):
                for k in range(ND):
                    mm = mm3(place[:, :], both(AT, ALL, k, ALL), both(xnT, ALL, k, slice(n * CH, n * CH + CH)), k == 0,
                             k == ND - 1)
                mm.then_inc(f_ready, 1)

            for i in range(TPC):
                tail_tile(i)
            for i in range(TPC):
                base_tile(i)
                tail_tile(TPC + i)
            inner(0, bankO)
            pe.wait_ge(f_lo, N_JOBS + 1)
            pe.wait_ge(xt_lo, 2 * NT)
            for k in range(ND):
                mm = pe.matmul(bankT[0][:, 0:E], xsum[:, k:k + 1].broadcast_to([P, P]), rwT[:, k, :],
                               start=(k == 0), stop=(k == ND - 1))
            mm.then_inc(f_ready, 1)
            inner(1, bankT[1])
            for i in range(TPC, NT):
                base_tile(i)
            for i in range(NT):
                if i % TPC == 0:
                    pe.wait_ge(f_lo, N_JOBS + 2 + i // TPC)
                rows = slice(i * P, (i + 1) * P)
                mm3(y_bank(NT + i), both(tT, ALL, rows), BT, True, True).then_inc(y_ready, 1)

        @block.scalar
        def _(act):
            def copy(place, src):
                return act.activation(place, src, ACT.Copy)

            def root(step, half):
                t = slice(half * TPC, (half + 1) * TPC)
                act.wait_ge(dve_step, 2 * step + 1)
                act.activation(std[:, 1, t], std[:, 0, t], ACT.Sqrt).then_inc(act_step, 1)

            def normalised_hi(made, tiles):
                for i in tiles:
                    act.wait_ge(xt_ready, made + i + 1)
                    copy(xnT[0][:, :, i * P:(i + 1) * P], bankT[i % 2][:, :].rearrange("p (k n) -> p k n", k=ND))\
                        .then_inc(xt_hi, 1)

            def weights_hi(no, slot, per_slot, places):
                act.wait_ge(w_loaded[slot], 16 * per_slot)
                place = places[0]
                src = stage[:, slot, 0:HD if places is Wlk else CH]
                if len(place.shape) == 3:
                    copy(place[:, :, :], src.rearrange("p (k n) -> p k n", k=ND)).then_inc(w_hi, 1)
                else:
                    copy(place[:, :], src).then_inc(w_hi, 1)

            def ffn_high(n):
                if n == 0:
                    act.wait_ge(scored, H * NW * TPC)
                act.wait_ge(f_ready, n + 1)
                src = four[n % 3]
                if n < ND:
                    copy(WT[0][:, n, :], src).then_inc(f_hi, 1)
                elif n == ND:
                    copy(AT[0], src.rearrange("p (k n) -> p k n", k=ND)).then_inc(f_hi, 1)
                else:
                    copy(BT[0], src).then_inc(f_hi, 1)

            def fetched(g, hh, name, places, at=None):
                no = load_no(0, hh, name) if at is None else at
                weights_hi(None, no % 2, g * (LOADS_PER_GROUP // 2) + (no // 2 + 1), places)

            def rope_take(n_x, no, slot, bank=0):
                if not (isinstance(no, int) and no < RING):
                    act.wait_ge(rope_lo, no - (RING - 1))
                act.wait_ge(x_ready, n_x)
                copy(rot[:, slot, :], banksX[bank] if isinstance(bank, int) else bank).then_inc(rope_raw, 1)

            def rope_high(no, slot, place):
                act.wait_ge(rope_sum, no + 1)
                copy(place, rot[:, slot, :]).then_inc(rope_hi, 1)

            def value_high(n_x, place, n, bank=0):
                act.wait_ge(x_ready, n_x)
                copy(place[:, n * TPC:(n + 1) * TPC, :], banksX[bank].rearrange("p (k n) -> p k n", k=TPC))\
                    .then_inc(v_hi, 1)

            def exp_tile(no, c, t):
                act.wait_ge(row_maxed, no + 1)
                act.activation(prob_tile(c, t), prob_tile(c, t), ACT.Exp, bias=nmax[:, c, t:t + 1], scale=-1.0,
                               accum_out=rsum[:, c, t:t + 1]).then_inc(exped, 1)

            def block_hi(g, hh, w, j):
                no = block_no(g, hh, w, j)
                c = WINDOWS[w][1]
                if not (isinstance(no, int) and no == 0):
                    ahead = 2 if (j < 2 or j == BLOCKS[w] - 1) else 1
                    act.wait_ge(pv_done, no - ahead + C_PV)
                else:
                    act.wait_ge(cleared, 1)
                act.wait_ge(transposed, n_transposed(g, hh, w, j))
                copy(pt_place(0, hh, w, j), bankT[j % 2][:, block_columns(c, j):CH]).then_inc(pt_hi, 1)

            highs = [{(0, 3): ("LK", 0), (1, 0): ("LK", 1), (3, 1): ("Q", 0), (3, 3): ("Q", 1)} for _ in range(GROUP)]
            highs[GROUP - 1].update({(2, 3): ("K", 0), (3, 0): ("K", 1)})

            def group_of_heads(g, last):
                for hh, w, more in windows(g, last):
                    nw, nhh = (w + 1) % NW, hh + (w == NW - 1)
                    kind, c = WINDOWS[w]
                    third = last and hh == GROUP - 1
                    for s in range(BLOCKS[w]):
                        name, n = pieces_of(w, hh, more).get(s, ("", 0))
                        if name == "LK":
                            rope_take(n_piece(g, hh, w, s), rope_no(g, hh, name, n), rope_no(0, hh, name, n) % RING,
                                      piece_bank(hh, w, s, more))
                        early = s + 2 < BLOCKS[w] and name in ("", "LK", "OUT0", "OUT1")
                        if early:
                            block_hi(g, hh, w, s + 2)
                        if more or w < NW - 1:
                            for t in range(TPC):
                                if TILE_SLOTS[w][t] == s:
                                    exp_tile(tiles_made(g, hh, w) + t, WINDOWS[nw][1], t)
                        if name in ("Q", "K"):
                            rope_take(n_piece(g, hh, w, s), rope_no(g, hh, name, n), rope_no(0, hh, name, n) % RING,
                                      piece_bank(hh, w, s, more))
                        if w == 1 and s in (3, 5):
                            if s == 3:
                                act.wait_ge(pv_done, last_block(g, hh, 0) + 1 + C_PV)
                            value_high(n_piece(g, hh, 1, s), LV[0], s // 5, piece_bank(hh, 1, s, more))
                        if w == 3 and s in (2, 3) and more and hh == GROUP - 1:
                            if s == 2:
                                act.wait_ge(pv_done, last_block(g, hh, 1) + 1 + C_PV)
                            value_high(n_piece(g, hh, 3, s), V[0], s - 2, piece_bank(hh, 3, s, more))
                        if s + 2 < BLOCKS[w] and not early:
                            block_hi(g, hh, w, s + 2)
                        if w == NW - 1 and not more and s < ND + 2:
                            ffn_high(s)
                        if (w, s) in highs[hh]:
                            name, n = highs[hh][w, s]
                            if (w, s) in ((0, 3), (2, 3), (3, 1)):
                                act.wait_ge(scored, tiles_made(g, hh, w))
                            if more or name == "LK":
                                place = {"LK": LKT[0][:, n * CH:(n + 1) * CH],
                                         "K": KT[0][:, n * CH:(n + 1) * CH],
                                         "Q": QT[0][:, (hh + 1) % 2, n * CH:(n + 1) * CH]}[name]
                                rope_high(rope_no(g, hh, name, n), rope_no(0, hh, name, n) % RING, place)
                        if w == 0 and s >= 2 and more and hh == GROUP - 1:
                            fetched(g, hh, *(("Wk", Wk), ("Wv", Wv))[s - 2])
                        if w == 1 and s == (4 if hh == GROUP - 1 else 1) and more:
                            act.wait_ge(x_ready, n_piece(g, hh, 0, 0))
                            fetched(g, hh, "Wq", Wq)
                        if w == 2 and s < 2:
                            if s == 0:
                                act.wait_ge(x_ready, n_piece(g, hh, 1, 7))
                            name, places = (("Wo", Wo), ("Wlo", Wlo))[s]
                            fetched(g, hh, name, places, load_no(0, hh, "Wk") + s if third else None)
                        if w == 3 and s in (5, 6) and more:
                            name, places = (("Wlk", Wlk), ("Wlv", Wlv))[s - 5]
                            fetched(g, hh, name, places)
                    for j in range(2):
                        if nhh < GROUP:
                            block_hi(g, nhh, nw, j)
                        elif more:
                            block_hi(g + 1, 0, 0, j)
                    act.wait_ge(x_ready, n_piece(g, hh, *((0, 0) if c == 0 else (1, 7))))
                    act.wait_ge(o_scaled, unit_no(g, hh, w) + 1 + C_OS)
                    copy(OT[0][:, kind, c * CH:(c + 1) * CH], o_raw[:, w % 2, :]).then_inc(o_hi, 1)

            weights_hi(0, 0, 1, Wq)
            weights_hi(1, 1, 1, Wk)
            root(0, 0)
            normalised_hi(0, range(TPC))
            weights_hi(2, 0, 2, Wlv)
            root(1, 1)

            def first_take(p):
                rope_take((1, 2, 5, 6)[p], p, p % RING, four[p % 2])

            def first_high(p):
                n = p // 2
                rope_high(p, p % RING, (QT[0][:, 0, n * CH:(n + 1) * CH], KT[0][:, n * CH:(n + 1) * CH])[p % 2])

            def first_latent(n):
                act.wait_ge(x_ready, 3 + 4 * n)
                copy(lqT[0][:, n * CH:(n + 1) * CH], four[2]).then_inc(v_hi, 1)

            normalised_hi(0, range(TPC, TPC + 2))
            weights_hi(3, 1, 2, Wv)
            first_take(0)
            normalised_hi(0, range(TPC + 2, NT))
            first_take(1)
            first_high(0)
            first_latent(0)
            first_high(1)
            first_take(2)
            first_take(3)
            first_latent(1)
            first_high(2)
            weights_hi(4, 0, 3, Wlk)
            for t in range(TPC):
                exp_tile(t, 0, t)
            first_high(3)
            weights_hi(5, 1, 3, Wlv)
            for n in range(2):
                value_high(9 + n, V[0], n, n)
            block_hi(0, 0, 0, 0)
            block_hi(0, 0, 0, 1)

            with act.Fori(0, KVH - 1) as g:
                group_of_heads(g, False)
            group_of_heads(KVH - 1, True)

            for half in range(2):
                root(2 + half, half)
                normalised_hi(NT, range(half * TPC, (half + 1) * TPC))
            act.wait_ge(f_free, 1)
            act.activation(soft[:, 2, :], soft[:, 0, :], ACT.Exp, bias=soft[:, 1, 0:1], scale=1.0,
                           accum_out=soft[:, 1, 1:2]).then_inc(act_step, 1)
            for n in range(2):
                act.wait_ge(f_free, 2 + n)
                copy(tT[0][:, n * CH:(n + 1) * CH], o_raw[:, n, :]).then_inc(f_hi, 1)

        @block.vector
        def _(dve):
            def statistics(step, half):
                tiles = range(half * TPC, (half + 1) * TPC)
                for i in tiles:
                    dve.bn_stats(stats[:, i, :], acc[:, i, :]).then_inc(dve_chain, 1)
                chain[0] += TPC
                dve.wait_ge(dve_chain, chain[0])
                for i in tiles:
                    dve.bn_aggr(mv[:, i, :], stats[:, i, :]).then_inc(dve_chain, 1)
                chain[0] += TPC
                dve.wait_ge(dve_chain, chain[0])
                t = slice(tiles[0], tiles[-1] + 1)
                dve.tensor_scalar(std[:, 0, t], mv[:, t, 1], EPS, None, ALU.add).then_inc(dve_step, 1)

            def inverse_std(step, half):
                t = slice(half * TPC, (half + 1) * TPC)
                dve.wait_ge(act_step, step + 1)
                link(dve.reciprocal(std[:, 2, t], std[:, 1, t]))
                link(dve.tensor_tensor(std[:, 3, t], std[:, 2, t], std[:, 0, t], ALU.mult))
                link(dve.tensor_tensor(std[:, 2, t], std[:, 3, t], std[:, 1, t], ALU.add))
                link(dve.tensor_scalar(std[:, 3, t], std[:, 2, t], 0.5, None, ALU.mult))
                dve.reciprocal(std[:, 2, t], std[:, 3, t]).then_inc(dve_step, 1)
                dve.wait_ge(dve_step, 2 * step + 2)

            chain = [0]
            dve_chain = f_chain

            def link(ins):
                chain[0] += 1
                ins.then_inc(dve_chain, 1)
                dve.wait_ge(dve_chain, chain[0])

            def normalise(made, i):
                if i >= 2:
                    dve.wait_ge(xt_ready, made + i - 1)
                    if made:
                        dve.wait_ge(xt_used, i - 1)
                dve.tensor_scalar(o_raw[:, i % 2, :], acc[:, i, :], mv[:, i, 0:1], std[:, 2, i:i + 1],
                                  ALU.subtract, ALU.mult).then_inc(xn_made, 1)

            def normalised_lo(made, i):
                dve.wait_ge(xt_hi, made + i + 1)
                rows = slice(i * P, (i + 1) * P)
                dve.tensor_tensor(xnT[1][:, :, rows], bankT[i % 2][:, :].rearrange("p (k n) -> p k n", k=ND),
                                  f32(xnT[0][:, :, rows]), ALU.subtract).then_inc(xt_lo, 1)

            def row_max(no, parity, c, t):
                dve.wait_ge(scored, no + 1)
                dve.sem_inc(score_seen, 1)
                width = P * (TPC * c + t + 1)
                place = tile_view(prob_tile(c, t), c)
                src = scores[parity][:, 0, 0:width] if c == 0 else scores[parity][:, :, 0:width // 2]
                dve.tensor_tensor_reduce(place, src, tile_view(mask[:, S - width:S], c), -SCALE, -MASKED,
                                         ALU.add, ALU.min, nmax[:, c, t:t + 1]).then_inc(row_maxed, 1)

            def block_lo(g, hh, w, j):
                c = WINDOWS[w][1]
                dve.wait_ge(pt_hi, block_no(g, hh, w, j) + 1)
                dve.tensor_tensor(pt_place(1, hh, w, j), bankT[j % 2][:, block_columns(c, j):CH],
                                  f32(pt_place(0, hh, w, j)), ALU.subtract).then_inc(pt_lo, 1)

            def rotate(no, slot, n, place=None):
                half = n if place is None else place
                if not (isinstance(no, int) and no < 2):
                    dve.wait_ge(rope_sum, no - 1)
                dve.wait_ge(rope_raw, no + 1)
                t = slice(n * CH, (n + 1) * CH)
                dve.tensor_tensor(rot_half[0:HALF, half, :], rot[HALF:HD, slot, :], sin[HALF:HD, t], ALU.mult)
                dve.tensor_tensor(rot_half[HALF:HD, half, :], rot[0:HALF, slot, :], sin[0:HALF, t], ALU.mult)\
                    .then_inc(rope_half, 1)

            def value_copy(n_x, n, bank=0):
                dve.wait_ge(x_ready, n_x)
                dve.tensor_copy(vT[:, n * CH:(n + 1) * CH], banksX[bank]).then_inc(x_free, 1)

            def value_lo(n_v, places, n, bank=0):
                dve.wait_ge(v_hi, n_v)
                rows = slice(n * TPC, (n + 1) * TPC)
                dve.tensor_tensor(places[1][:, rows, :], banksX[bank].rearrange("p (k n) -> p k n", k=TPC),
                                  f32(places[0][:, rows, :]), ALU.subtract).then_inc(x_free, 1)

            def add_out(n_x, n_taken, i, bank=0):
                dve.wait_ge(x_ready, n_x)
                dve.wait_ge(x_free, n_taken - 1)
                dve.tensor_tensor(acc[:, i, :], banksX[bank], acc[:, i, :], ALU.add).then_inc(x_free, 1)

            def piece(g, hh, w, s, name, n, bank):
                n_x = n_piece(g, hh, w, s)
                if name in ROPE:
                    rotate(rope_no(g, hh, name, n), rope_no(0, hh, name, n) % RING, n)
                elif name in ("V", "LV"):
                    value_copy(n_x, n, bank)
                elif name in ("VT", "LVT"):
                    value_lo(vt_no(g, hh, name, n) + 3, V if name == "VT" else LV, n, bank)
                else:
                    add_out(n_x, n_free(g, hh, w, s), n + (TPC if name == "OUT1" else 0), bank)

            def ffn_low(n):
                src = four[n % 3]
                if n < ND + 2:
                    dve.wait_ge(f_hi, n + 1)
                    if n < ND:
                        hi, lo = f32(WT[0][:, n, :]), WT[1][:, n, :]
                    elif n == ND:
                        hi, lo = f32(AT[0]), AT[1]
                        src = src.rearrange("p (k n) -> p k n", k=ND)
                    else:
                        hi, lo = f32(BT[0]), BT[1]
                    dve.tensor_tensor(lo, src, hi, ALU.subtract).then_inc(f_lo, 1)
                else:
                    dve.wait_ge(f_ready, n + 1)
                    dve.tensor_copy(rwT, src[:, 0:ND * E].rearrange("p (k e) -> p k e", k=ND)).then_inc(f_lo, 1)

            def scale_out(g, hh, w):
                unit = unit_no(g, hh, w)
                kind, c = WINDOWS[w]
                dve.wait_ge(o_lo[c], n_out_low(g, hh, kind) - 1)
                dve.wait_ge(pv_done, last_block(g, hh, w) + 1 + C_PV)
                dve.wait_ge(inverses_loaded, 16 * (unit + 1))
                dve.tensor_tensor(o_raw[:, w % 2, :].rearrange("p (t q) -> p t q", q=P),
                                  bankO[:, :].rearrange("p (t q) -> p t q", q=P),
                                  inv_b[:, w % 2, :].rearrange("p (q t) -> p t q", q=P), ALU.mult).then_inc(o_scaled, 1)

            def out_low(g, hh, w):
                kind, c = WINDOWS[w]
                dve.wait_ge(o_hi, unit_no(g, hh, w) + 1)
                t = slice(c * CH, (c + 1) * CH)
                dve.tensor_tensor(OT[1][:, kind, t], o_raw[:, w % 2, :], f32(OT[0][:, kind, t]), ALU.subtract)\
                    .then_inc(o_lo[0], 1)

            def group_of_heads(g, last):
                for hh, w, more in windows(g, last):
                    nw, nhh = (w + 1) % NW, hh + (w == NW - 1)
                    c = WINDOWS[w][1]
                    for s in range(BLOCKS[w]):
                        if s == 0:
                            dve.wait_ge(exped, tiles_made(g, hh, w))
                            dve.reciprocal(rinv[:, c, :], rsum[:, c, :]).then_inc(inverted, 1)
                        if more or w < NW - 1:
                            for t in range(TPC):
                                if TILE_SLOTS[w][t] == s:
                                    if t == 0:
                                        dve.wait_ge(transposed, block_no(g, hh, w, 0) + C_T)
                                    row_max(tiles_made(g, hh, w) + t, t % 2, WINDOWS[nw][1], t)
                        here = pieces_of(w, hh, more)
                        if s in here and here[s][0] not in ("LK", "K"):
                            piece(g, hh, w, s, *here[s], piece_bank(hh, w, s, more))
                        if s + 2 < BLOCKS[w]:
                            block_lo(g, hh, w, s + 2)
                        if w == NW - 1 and not more and s < N_JOBS:
                            ffn_low(s)
                        if here.get(s - 1, ("", 0))[0] in ("LK", "K"):
                            piece(g, hh, w, s - 1, *here[s - 1], piece_bank(hh, w, s - 1, more))
                    for j in range(2):
                        if j == 1:
                            scale_out(g, hh, w)
                        if nhh < GROUP:
                            block_lo(g, nhh, nw, j)
                        elif more:
                            block_lo(g + 1, 0, 0, j)
                    if c == 0:
                        out_low(g, hh, w)

            dve.sem_inc(o_scaled, C_OS)
            dve.sem_inc(o_lo[0], C_OL)
            dve.wait_ge(x_loaded[0], 16)
            statistics(0, 0)
            inverse_std(0, 0)
            normalise(0, 0)
            normalise(0, 1)
            for i in range(TPC):
                normalised_lo(0, i)
                if i < 2:
                    normalise(0, i + 2)
            dve.wait_ge(x_loaded[1], 16)
            statistics(1, 1)
            inverse_std(1, 1)
            normalise(0, 4)
            normalise(0, 5)
            dve.wait_ge(consts_loaded, 48)
            dve.tensor_copy(mask[:, :], vT[:, :]).then_inc(mask_made, 1)

            def latent_lo(n):
                dve.wait_ge(v_hi, n + 1)
                dve.tensor_tensor(lqT[1][:, n * CH:(n + 1) * CH], four[2], f32(lqT[0][:, n * CH:(n + 1) * CH]),
                                  ALU.subtract).then_inc(x_free, 1)

            normalised_lo(0, 4)
            normalised_lo(0, 5)
            rotate(0, 0, 0, 0)
            normalise(0, 6)
            normalise(0, 7)
            normalised_lo(0, 6)
            normalised_lo(0, 7)
            rotate(1, 1, 0, 1)
            latent_lo(0)
            dve.wait_ge(mask_made, 1)
            value_copy(4, 0, 1)
            rotate(2, 2, 1, 0)
            rotate(3, 0, 1, 1)
            latent_lo(1)
            value_copy(8, 1, 1)
            for t in range(TPC):
                row_max(t, t % 2, 0, t)
            for n in range(2):
                value_lo(3 + n, V, n, n)
            block_lo(0, 0, 0, 0)
            block_lo(0, 0, 0, 1)

            with dve.Fori(0, KVH - 1) as g:
                group_of_heads(g, False)
            group_of_heads(KVH - 1, True)

            def last_add(n):
                add_out(n_piece(KVH - 1, GROUP - 1, 3, 7) + n + 1, n_free(KVH - 1, GROUP - 1, 3, 7) + n + 1, TPC + n, n % 2)

            def add_y(n):
                i = n % NT
                dve.wait_ge(y_ready, n + 1)
                dve.wait_ge(*((y_biased, i + 1) if n < NT else (y_added, i + 1)))
                dve.tensor_tensor(acc[:, i, :], four[n % 4], acc[:, i, :], ALU.add).then_inc(y_added, 1)

            dve.wait_ge(x_free, n_free(KVH - 1, GROUP - 1, 3, 7))
            statistics(2, 0)
            last_add(0)
            inverse_std(2, 0)
            normalise(NT, 0)
            normalise(NT, 1)
            last_add(1)
            last_add(2)
            last_add(3)
            normalised_lo(NT, 0)
            normalise(NT, 2)
            normalised_lo(NT, 1)
            normalise(NT, 3)
            dve.wait_ge(x_free, n_free(KVH - 1, GROUP - 1, 3, 7) + TPC)
            statistics(3, 1)
            normalised_lo(NT, 2)
            normalised_lo(NT, 3)
            inverse_std(3, 1)
            for i in range(TPC):
                normalise(NT, TPC + i)
                if i:
                    normalised_lo(NT, TPC + i - 1)
                    add_y(i - 1)
            normalised_lo(NT, NT - 1)
            dve.wait_ge(xt_used, NT)
            dve.tensor_scalar(xsum, bankX[:, 0:ND], 1.0 / (Q_STOP - Q_START), None, ALU.mult).then_inc(f_lo, 1)
            add_y(TPC - 1)
            dve.wait_ge(f_ready, N_JOBS + 2)
            link(dve.tensor_tensor(soft[:, 0, :], bankT[0][:, 0:E], r_bias, ALU.add))
            link(dve.tensor_reduce(soft[:, 1, 2:3], soft[:, 0, :], AX.X, ALU.max))
            dve.tensor_scalar(soft[:, 1, 0:1], soft[:, 1, 2:3], -1.0, None, ALU.mult).then_inc(f_free, 1)
            dve.wait_ge(act_step, 5)
            link(dve.reciprocal(soft[:, 1, 3:4], soft[:, 1, 1:2]))
            link(dve.tensor_tensor(soft[:, 3, :], soft[:, 2, :], pick, ALU.mult))
            link(dve.tensor_reduce(soft[:, 4, 0:1], soft[:, 3, :], AX.X, ALU.add))
            link(dve.tensor_scalar(soft[:, 4, 1:2], soft[:, 4, 0:1], soft[:, 1, 3:4], LORA_SCALING, ALU.mult, ALU.mult))
            for n, src in enumerate((bankO, bankT[1])):
                dve.wait_ge(f_ready, N_JOBS + 1 + 2 * n)
                dve.tensor_scalar(o_raw[:, n, :], src[:, :], soft[:, 4, 1:2], None, ALU.mult).then_inc(f_free, 1)
            for n in range(2):
                dve.wait_ge(f_hi, ND + 3 + n)
                t = slice(n * CH, (n + 1) * CH)
                dve.tensor_tensor(tT[1][:, t], o_raw[:, n, :], f32(tT[0][:, t]), ALU.subtract).then_inc(f_lo, 1)
            for n in range(TPC, 2 * NT):
                add_y(n)

        @block.gpsimd
        def _(pool):
            def subtract(place, src, hi):
                return pool.tensor_tensor(place, src, f32(hi), ALU.subtract)

            def rope_add(no, slot, n, place=None):
                half = n if place is None else place
                pool.wait_ge(rope_half, no + 1)
                pool.tensor_tensor(rot[:, slot, :], rot[:, slot, :], cos[:, chunk(n)], ALU.mult).then_inc(rope_cos, 1)
                pool.wait_ge(rope_cos, no + 1)
                pool.tensor_tensor(rot[:, slot, :], rot[:, slot, :], rot_half[:, half, :], ALU.add).then_inc(rope_sum, 1)

            def rope_low(no, slot, places, at):
                pool.wait_ge(rope_hi, no + 1)
                subtract(places[1][at], rot[:, slot, :], places[0][at]).then_inc(rope_lo, 1)

            def weights_low(no, slot, places):
                pool.wait_ge(w_hi, no + 1)
                src = stage[:, slot, 0:HD if places is Wlk else CH]
                if len(places[0].shape) == 3:
                    subtract(places[1][:, :, :], src.rearrange("p (k n) -> p k n", k=ND), places[0][:, :, :])\
                        .then_inc(w_lo, 1)
                else:
                    subtract(places[1][:, :], src, places[0][:, :]).then_inc(w_lo, 1)

            def ropes(g, hh, name, places, at):
                for n in range(2):
                    rope_add(rope_no(g, hh, name, n), rope_no(0, hh, name, n) % RING, n)
                for n in range(2):
                    rope_low(rope_no(g, hh, name, n), rope_no(0, hh, name, n) % RING, places, at(n))

            ALL = slice(None)

            def chunk(n):
                return slice(n * CH, (n + 1) * CH)

            def out_low(g, hh, w):
                kind, c = WINDOWS[w]
                pool.wait_ge(o_hi, unit_no(g, hh, w) + 1)
                at = (ALL, kind, chunk(c))
                subtract(OT[1][at], o_raw[:, w % 2, :], OT[0][at]).then_inc(o_lo[1], 1)

            def group_of_heads(g, last):
                for hh, w, more in windows(g, last):
                    if w == 0:
                        ropes(g, hh, "LK", LKT, lambda n: (ALL, chunk(n)))
                        if more and hh == GROUP - 1:
                            for name, places in (("Wk", Wk), ("Wv", Wv)):
                                weights_low(load_no(g, hh, name), load_no(0, hh, name) % 2, places)
                    if w == 1 and more:
                        weights_low(load_no(g, hh, "Wq"), load_no(0, hh, "Wq") % 2, Wq)
                    if w == 1:
                        out_low(g, hh, w)
                    if w == 2:
                        no, at = ((load_no(g, hh, "Wo"), load_no(0, hh, "Wo")) if more else
                                  (load_no(g, hh, "Wk"), load_no(0, hh, "Wk")))
                        for k, places in enumerate((Wo, Wlo)):
                            weights_low(no + k, (at + k) % 2, places)
                    q_at = lambda n: (ALL, (hh + 1) % 2, chunk(n))
                    if w == 2 and more:
                        k_no = [(rope_no(g, hh, "K", n), rope_no(0, hh, "K", n) % RING) for n in range(2)]
                        if hh == GROUP - 1:
                            rope_add(*k_no[0], 0)
                            rope_add(*k_no[1], 1)
                            rope_low(*k_no[0], KT, (ALL, chunk(0)))
                        rope_add(rope_no(g, hh, "Q", 0), rope_no(0, hh, "Q", 0) % RING, 0)
                        if hh == GROUP - 1:
                            rope_low(*k_no[1], KT, (ALL, chunk(1)))
                    if w == 3 and more:
                        rope_low(rope_no(g, hh, "Q", 0), rope_no(0, hh, "Q", 0) % RING, QT, q_at(0))
                        rope_add(rope_no(g, hh, "Q", 1), rope_no(0, hh, "Q", 1) % RING, 1)
                        rope_low(rope_no(g, hh, "Q", 1), rope_no(0, hh, "Q", 1) % RING, QT, q_at(1))
                        for name, places in (("Wlk", Wlk), ("Wlv", Wlv)):
                            weights_low(load_no(g, hh, name), load_no(0, hh, name) % 2, places)
                    if w == 3:
                        out_low(g, hh, w)

            pool.sem_inc(o_lo[1], C_OL)
            weights_low(0, 0, Wq)
            weights_low(1, 1, Wk)
            for tensor in (*PTD, *OT, *Wo, *Wlo):
                flat = tensor[tuple([ALL] * len(tensor.shape))]
                ins = pool.memset(f32(flat), 0.0)
            ins.then_inc(cleared, 1)
            weights_low(2, 0, Wlv)
            weights_low(3, 1, Wv)
            for p in range(ROPES_BEFORE):
                n = p // 2
                rope_add(p, p % RING, n, p % 2)
                rope_low(p, p % RING, (QT, KT)[p % 2], ((ALL, 0, chunk(n)), (ALL, chunk(n)))[p % 2])
            weights_low(4, 0, Wlk)
            weights_low(5, 1, Wlv)

            with pool.Fori(0, KVH - 1) as g:
                group_of_heads(g, False)
            group_of_heads(KVH - 1, True)

            pool.wait_ge(router_loaded, 16 * 4)
            for i in range(NT):
                pool.wait_ge(xn_made, NT + i + 1)
                pool.tensor_tensor(acc[:, i, :], acc[:, i, :], bias, ALU.add).then_inc(y_biased, 1)


_INS = ["L0_attn_hidden_states", "L0_attn_w_q", "L0_attn_w_k", "L0_attn_w_v", "L0_attn_w_o", "L0_attn_w_lq",
        "L0_attn_w_lk", "L0_attn_w_lv", "L0_attn_w_lo", "L0_ffn_W", "L0_ffn_b", "L0_ffn_A", "L0_ffn_B",
        "L0_ffn_router_W", "L0_ffn_router_b"]


def shape_constants():
    inv_freq = (1.0 / THETA ** (np.arange(0, HD, 2, dtype=np.float32) / HD)).astype(np.float32)
    freqs = np.outer(np.arange(S, dtype=np.float32), inv_freq).astype(np.float32)
    cos = np.tile(np.cos(freqs).T, (2, 1)).astype(np.float32)
    sin = np.concatenate([np.sin(freqs).T, -np.sin(freqs).T], 0).astype(np.float32)
    mask = np.zeros((P, S), np.float32)
    mask[:, S - P:] = np.where(np.tril(np.ones((P, P), bool)), 0.0, MASKED)
    pick = (np.arange(P)[:, None] // R == np.arange(E)[None, :]).astype(np.float32)
    token = np.arange(NT)[None, :] * P + np.arange(P)[:, None]
    averaged = ((token >= Q_START) & (token < Q_STOP)).astype(np.float32)
    return {"cos": cos, "sin": sin, "mask": mask, "ident": np.eye(P, dtype=np.float32), "pick": pick,
            "averaged": averaged}


def kernel(**inputs):
    import concourse.bacc as bacc
    from concourse.bass_utils import run_bass_kernel_spmd

    nc = bacc.Bacc("TRN2", target_bir_lowering=False, num_devices=1, dynamic_dma_scratch_size=1024)
    arrays, args = {}, []
    for name in _INS:
        arrays[f"in_{name}"] = np.ascontiguousarray(inputs[name])
    for name, a in shape_constants().items():
        arrays[f"const_{name}"] = np.ascontiguousarray(a)
    for name, a in arrays.items():
        args.append(nc.dram_tensor(name, a.shape, mybir.dt.from_np(a.dtype), kind="ExternalInput").ap())
    args.append(nc.dram_tensor("out", (1, S, D), F32, kind="ExternalOutput").ap())
    args.append(nc.dram_tensor("inverses", (2, CH), F32, kind="Internal").ap())
    attn_ffn_kernel(nc, *args)
    result = run_bass_kernel_spmd(nc, [arrays], core_ids=[0])
    return result.results[0]["out"]
```
